# Optimizing a Trainium2 kernel written in Bass

```python
import numpy as np
import jax
import jax.numpy as jnp

def _softmax(x, axis=-1):
    return jax.nn.softmax(x, axis=axis)

def _gelu(x):
    return jax.nn.gelu(x, approximate=True)

def _silu(x):
    return jax.nn.silu(x)

def _sigmoid(x):
    return jax.nn.sigmoid(x)

def _layernorm(x, axis=-1, eps=1e-05):
    m = jnp.mean(x, axis=axis, keepdims=True)
    v = jnp.var(x, axis=axis, keepdims=True)
    return (x - m) / jnp.sqrt(v + eps)

def _scatter_add(tgt, idx, src, axis=0):
    return tgt.at[idx].add(src)

def _segment_sum(src, seg, n):
    return jax.ops.segment_sum(src, seg, n)
kernel_name = 'mk_prb_d1_jaxref_r4_4993da'

def setup_inputs(seed: int=0):
    np.random.seed(seed)
    _w = jnp.asarray

    def _L0_attn_setup():
        import jax, jax.numpy as jnp
        import numpy as np
        EMBED_DIM = 256
        NUM_HEADS = 16
        HEAD_DIM = EMBED_DIM // NUM_HEADS
        LN_EPS = 1e-05

        def _layernorm(x, g, b):
            mu = jnp.mean(x, axis=-1, keepdims=True)
            var = jnp.mean(jnp.square(x - mu), axis=-1, keepdims=True)
            return (x - mu) * jax.lax.rsqrt(var + LN_EPS) * g + b
        key = jax.random.key(seed)
        ks = jax.random.split(key, 5)
        N, L, C = (32, 577, EMBED_DIM)
        x = jax.random.normal(ks[0], (N, L, C), dtype=jnp.float32)
        ln1_g = jnp.ones((C,), dtype=jnp.float32)
        ln1_b = jnp.zeros((C,), dtype=jnp.float32)
        w_in = jax.random.normal(ks[1], (3 * C, C), dtype=jnp.float32) * C ** (-0.5)
        b_in = jax.random.normal(ks[2], (3 * C,), dtype=jnp.float32) * 0.02
        w_out = jax.random.normal(ks[3], (C, C), dtype=jnp.float32) * C ** (-0.5)
        b_out = jax.random.normal(ks[4], (C,), dtype=jnp.float32) * 0.02
        return {'x': x, 'ln1_g': ln1_g, 'ln1_b': ln1_b, 'w_in': w_in, 'b_in': b_in, 'w_out': w_out, 'b_out': b_out}
    _L0_attn_in = _L0_attn_setup()

    def _L0_ffn_setup():
        import jax, jax.numpy as jnp
        import numpy as np
        EMB = 256
        FF = 4 * EMB

        def _ternary(w):
            scale = jnp.maximum(jnp.mean(jnp.abs(w)), 1e-08)
            w_t = jnp.clip(jnp.round(w / scale), -1.0, 1.0)
            return w + jax.lax.stop_gradient(w_t - w)
        key = jax.random.key(seed)
        kx, k1, k2, kb1, kb2 = jax.random.split(key, 5)
        x = jax.random.normal(kx, (4, 512, EMB), dtype=jnp.float32)
        lim1 = 1.0 / np.sqrt(EMB)
        lim2 = 1.0 / np.sqrt(FF)
        W1 = jax.random.uniform(k1, (FF, EMB), jnp.float32, -lim1, lim1)
        b1 = jax.random.uniform(kb1, (FF,), jnp.float32, -lim1, lim1)
        W2 = jax.random.uniform(k2, (EMB, FF), jnp.float32, -lim2, lim2)
        b2 = jax.random.uniform(kb2, (EMB,), jnp.float32, -lim2, lim2)
        return {'x': x, 'W1': W1, 'b1': b1, 'W2': W2, 'b2': b2}
    _L0_ffn_in = _L0_ffn_setup()
    _d = {'L0_attn_x': _L0_attn_in['x'], 'L0_attn_ln1_g': _L0_attn_in['ln1_g'], 'L0_attn_ln1_b': _L0_attn_in['ln1_b'], 'L0_attn_w_in': _L0_attn_in['w_in'], 'L0_attn_b_in': _L0_attn_in['b_in'], 'L0_attn_w_out': _L0_attn_in['w_out'], 'L0_attn_b_out': _L0_attn_in['b_out'], 'L0_ffn_W1': _L0_ffn_in['W1'], 'L0_ffn_b1': _L0_ffn_in['b1'], 'L0_ffn_W2': _L0_ffn_in['W2'], 'L0_ffn_b2': _L0_ffn_in['b2']}
    _x0 = _d['L0_attn_x']
    _d['L0_attn_x'] = jax.random.normal(jax.random.fold_in(jax.random.key(seed), 1), (2, 2048, 256), dtype=_x0.dtype)
    del _x0
    return _d

def reference(L0_attn_x, L0_attn_ln1_g, L0_attn_ln1_b, L0_attn_w_in, L0_attn_b_in, L0_attn_w_out, L0_attn_b_out, L0_ffn_W1, L0_ffn_b1, L0_ffn_W2, L0_ffn_b2):

    def _L0_attn_ref(x, ln1_g, ln1_b, w_in, b_in, w_out, b_out):
        import jax, jax.numpy as jnp
        import numpy as np
        EMBED_DIM = 256
        NUM_HEADS = 16
        HEAD_DIM = EMBED_DIM // NUM_HEADS
        LN_EPS = 1e-05

        def _layernorm(x, g, b):
            mu = jnp.mean(x, axis=-1, keepdims=True)
            var = jnp.mean(jnp.square(x - mu), axis=-1, keepdims=True)
            return (x - mu) * jax.lax.rsqrt(var + LN_EPS) * g + b
        N, L, C = x.shape
        H, D = (NUM_HEADS, HEAD_DIM)
        z = _layernorm(x, ln1_g, ln1_b)
        qkv = z @ w_in.T + b_in
        q, k, v = jnp.split(qkv, 3, axis=-1)
        k = q

        def heads(t):
            return t.reshape(N, L, H, D).transpose(0, 2, 1, 3)
        q, k, v = (heads(q), heads(k), heads(v))
        scale = 1.0 / np.sqrt(D).astype(np.float32)
        scores = jnp.einsum('nhld,nhsd->nhls', q, k) * scale
        attn = jax.nn.softmax(scores, axis=-1)
        out = jnp.einsum('nhls,nhsd->nhld', attn, v)
        out = out.transpose(0, 2, 1, 3).reshape(N, L, C)
        return out @ w_out.T + b_out

    def _L0_ffn_ref(x, W1, b1, W2, b2):
        import jax, jax.numpy as jnp
        import numpy as np
        EMB = 256
        FF = 4 * EMB

        def _ternary(w):
            scale = jnp.maximum(jnp.mean(jnp.abs(w)), 1e-08)
            w_t = jnp.clip(jnp.round(w / scale), -1.0, 1.0)
            return w + jax.lax.stop_gradient(w_t - w)
        h = jnp.einsum('bsd,fd->bsf', x, _ternary(W1)) + b1
        h = jax.nn.gelu(h, approximate=False)
        out = jnp.einsum('bsf,df->bsd', h, _ternary(W2)) + b2
        return out
    x = L0_attn_x
    xn = _layernorm(x, axis=-1)
    x = x + _L0_attn_ref(xn, L0_attn_ln1_g, L0_attn_ln1_b, L0_attn_w_in, L0_attn_b_in, L0_attn_w_out, L0_attn_b_out) + _L0_ffn_ref(xn, L0_ffn_W1, L0_ffn_b1, L0_ffn_W2, L0_ffn_b2)
    return x

_drawn_inputs = setup_inputs


def setup_inputs(seed=0):
    import zlib

    import numpy as np

    out = dict(_drawn_inputs(seed))
    spreads = {'L0_attn_ln1_g': (1.0, 0.6), 'L0_attn_ln1_b': (0.0, 0.8)}
    factors = {'L0_attn_w_in': 8.0,
     'L0_attn_b_in': 8.0,
     'L0_attn_w_out': 8.0,
     'L0_attn_b_out': 64.0,
     'L0_ffn_b1': 25.32,
     'L0_ffn_b2': 64.0}
    for name, (base, spread) in spreads.items():
        noise = np.random.default_rng([zlib.crc32(name.encode()), seed]).standard_normal(out[name].shape)
        drawn = base * np.exp(spread * noise) if base else spread * noise
        out[name] = jnp.asarray(drawn.astype(out[name].dtype))
    for name, factor in factors.items():
        out[name] = (out[name] * factor).astype(out[name].dtype)
    return out
```

```python
from contextlib import ExitStack

import concourse.bass as bass
from concourse import mybir

F32 = mybir.dt.float32
BF16 = mybir.dt.bfloat16
ALU = mybir.AluOpType
ACT = mybir.ActivationFunctionType
AX = mybir.AxisListType
ds = bass.ds

P = 128
EPS = 1e-5
BANK = 512

KEY_PARTS = (0, 1, 2, 0, 1, 0)
QRY_PARTS = (0, 0, 0, 1, 1, 2)
A_PLAN = (3, 2, 3, 2, 3, 2, 3, 2, 3, 2, 3, 2, 2, 0, 0, 0)
ROT = 3


def wait(eng, sem, value):
    if not isinstance(value, int) or value > 0:
        eng.wait_ge(sem, value)


def attention_ffn(nc, x, ln_g, ln_b, wq_t, wv_t, wo_t, bq, bv, bo, w1_t, b1, w2_t, b2, ident, out):
    NB, L, C = x.shape
    FF = w1_t.shape[1]
    D = 16
    H = C // D
    NH = NB * H
    KC = C // P
    KF = FF // P
    NBLK = L // P
    NCH = L // BANK
    TG = BANK // P
    NT = NB * L // P
    NG = NT // TG
    GB = NG // NB
    HC = P // D
    NHALF = 2 * NBLK
    NE = NBLK * NCH
    SPLIT = len(KEY_PARTS) * D
    KROWS = SPLIT + 2
    W = 2 * BANK
    SCALE = 1.0 / float(D) ** 0.5
    assert NCH == 4 and sum(A_PLAN) == NHALF and len(A_PLAN) == NBLK and (NH - 2) % ROT == 0

    x_v = x.rearrange("b (g t p) c -> (b g) p t c", t=TG, p=P)
    out_v = out.rearrange("b (g t p) c -> (b g) p t c", t=TG, p=P)
    q_dram = nc.dram_tensor("q_parts", (3, C, NB * L), BF16, kind="Internal").ap()
    o_dram = nc.dram_tensor("o_heads", (NH, NCH, 2 * D, BANK), F32, kind="Internal").ap()
    r_dram = nc.dram_tensor("o_recip", (NH, NCH, BANK), F32, kind="Internal").ap()

    ctx = ExitStack()
    with ctx:
        def sb(name, shape, dt=F32):
            return ctx.enter_context(nc.sbuf_tensor(name, shape, dt))

        def sem(name):
            return ctx.enter_context(nc.semaphore(name))

        wq = sb("wq", [P, KC, C]); wv = sb("wv", [P, KC, C]); wo = sb("wo", [P, KC, C])
        w1 = sb("w1", [P, KC * FF]); w2 = sb("w2", [P, KF * C])
        w1t = sb("w1_ternary", [P, KC, FF], BF16)
        w2t = sb("w2_ternary", [P, KF, C])
        idf = sb("ident_f32", [P, P]); idb = sb("ident_bf16", [P, P], BF16)
        ones = sb("ones", [P, P])
        g_col = sb("g_col", [P, KC]); b_col = sb("b_col", [P, KC])
        bq_col = sb("bq_col", [P, KC]); b1_col = sb("b1_col", [P, KF])
        bv_row = sb("bv_row", [P, C]); bo_row = sb("bo_row", [P, C]); b2_row = sb("b2_row", [P, C])
        bias_row = sb("bias_row", [P, C])
        wabs = sb("wabs", [P, 2]); thr = sb("thr", [P, 2]); half = sb("half", [P, 2]); nhalf = sb("nhalf", [P, 2])
        expo = sb("minus_half", [P, TG])
        xin = sb("xin", [P, TG, C]); xn = sb("xn", [P, TG, C]); zn = sb("zn", [P, TG, C])
        stats = sb("stats", [P, TG, 6]); mv = sb("mean_var", [P, TG, 2])
        carrier = sb("wait_carrier", [P, 1])
        eps = sb("eps", [P, TG])
        veps = sb("var_eps", [P, TG]); rstd = sb("rstd", [P, TG])
        x1 = sb("x1", [P, KC, BANK], BF16); x2 = sb("x2", [P, KC, BANK], BF16); x3 = sb("x3", [P, KC, BANK], BF16)
        xr = sb("x_rest", [P, KC, BANK])
        zt = sb("zt", [P, KC, BANK])
        qf = sb("qf", [P, KC, BANK]); qr = sb("q_rest", [P, KC, BANK])
        qp = sb("q_split", [P, KC, 3, BANK], BF16)
        hid = sb("hidden", [P, KF, BANK])
        below = hid[:, 0:KC * FF // BANK, :].rearrange("p f n -> p (f n)")
        f2 = sb("ffn_out", [P, TG, C])
        resid = sb("resid", [P, NT, C])
        v_all = sb("v_all", [P, NT, C])
        key = [sb(f"key{i}", [P, L], BF16) for i in range(ROT)]
        qry = [sb(f"qry{i}", [P, L], BF16) for i in range(ROT)]
        vst = sb("v_ones", [P, NBLK, 2 * D])
        prob = [w1, w2]
        part_max = sb("part_max", [P, NBLK, 2]); neg_max = sb("neg_max", [P, NBLK])
        max_split = sb("max_split", [P, 2, NBLK], BF16)
        max_rows = sb("max_rows", [2 * NBLK, P], BF16)
        o_sb, sums, rsum = (z[:, 0:2, :].rearrange("p t c -> p (t c)") for z in (xin, xn, zn))
        ot = [key[i][:, :].bitcast(F32).rearrange("p (k n) -> p k n", k=KC) for i in range(2)]
        rb = [qry[i][:, :].bitcast(F32).rearrange("p (k n) -> p k n", k=KC) for i in range(2)]
        on = [prob[i][:, 0:KC * BANK].rearrange("p (k n) -> p k n", k=KC) for i in range(2)]
        y = [prob[i][:, KC * BANK:2 * KC * BANK].rearrange("p (t c) -> p t c", t=TG) for i in range(2)]

        ps = ctx.enter_context(nc.psum_tensor("ps", [P, 8 * BANK], F32))

        def bank(b, n=1):
            return ps[:, b * BANK:(b + n) * BANK]
        tr_x = [bank(0), bank(1)]
        tr_z = [bank(2), bank(3)]
        pq = [bank(4), bank(5)]
        pf = [bank(6), bank(7)]
        pa = [bank(0, 2), bank(2, 2)]
        pb = [bank(4), bank(5)]
        pv = bank(6)
        pm = bank(7)[:, 0:P // 2].bitcast(BF16)
        py = [bank(0), bank(1)]

        s_w = sem("weights_loaded"); s_c = sem("constants"); s_x = sem("x_loaded")
        s_wd = sem("weight_dve"); s_wp = sem("weight_pe")
        s_ln = sem("ln_dve"); s_rs = sem("ln_pool"); s_xb = sem("x_plus_bias")
        s_tr = sem("transposed"); s_x1 = sem("x1"); s_xr = sem("x_rest_done"); s_x2 = sem("x2"); s_x3 = sem("x3")
        s_z = sem("zt_done"); s_q = sem("q_psum"); s_qa = sem("q_biased"); s_qr = sem("q_rest_done")
        s_q2 = sem("q2"); s_q3 = sem("q3"); s_qs = sem("q_stored"); s_v = sem("v_psum"); s_vd = sem("v_done")
        s_h = sem("hidden_psum"); s_g = sem("gelu_done"); s_f = sem("ffn_psum"); s_fe = sem("ffn_evacuated")
        s_ra = sem("resid_done")
        s_ld = [sem(f"head_loaded{i}") for i in range(ROT)]; s_a = sem("pass_a"); s_r = sem("row_max"); s_m = sem("max_dve")
        s_mt = sem("max_transposed"); s_mc = sem("max_copied"); s_mr = sem("max_rows_in_place")
        s_b = sem("pass_b"); s_e = sem("exp_done"); s_vs = sem("v_staged"); s_pv = sem("pv_done")
        s_o = sem("o_evacuated"); s_os = sem("o_stored")
        s_sl = sem("sums_loaded"); s_rc = sem("recip_done"); s_rw = sem("recip_stored")
        s_ol = [sem(f"o_loaded{i}") for i in range(2)]; s_on = sem("o_normalised"); s_y = sem("y_psum"); s_yd = sem("y_done")
        s_out = [sem(f"out_stored{i}") for i in range(2)]
        N_W = 13
        N_CONST = ROT + 6

        def a_half(eng, h, v, a):
            n = a % 2
            wait(eng, s_r, NHALF * h + a - 1)
            blk, half_ = a // 2, a % 2
            for j in range(2):
                col = half_ * W + j * BANK
                mm = eng.matmul(pa[n][:, j * BANK:(j + 1) * BANK], key[v][0:SPLIT, blk * P:(blk + 1) * P],
                                qry[v][0:SPLIT, col:col + BANK], start=True, stop=True)
            mm.then_inc(s_a, 1)

        def max_transpose(eng, h):
            eng.wait_ge(s_m, 3 * h + 3)
            wait(eng, s_mc, h)
            eng.transpose(pm[0:2 * NBLK, 0:P], max_split[:, :, :].rearrange("p s k -> p (s k)"), idb[:, :]).then_inc(s_mt, 1)

        def pv_block(eng, h, kb):
            eng.wait_ge(s_e, NE * h + NCH * (kb + 1))
            if kb % (NBLK // 2) == 0:
                eng.wait_ge(s_vs, 2 * h + 1 + kb // (NBLK // 2))
            if kb == 0:
                wait(eng, s_o, h)
            for c in range(NCH):
                mm = eng.matmul(pv[32 * c:32 * c + 2 * D, :], vst[:, kb, :],
                                prob[kb % 2][:, c * BANK:(c + 1) * BANK],
                                start=(kb == 0), stop=(kb == NBLK - 1))
            mm.then_inc(s_pv, 1)

        def b_chunk(eng, h, v, kb, c):
            i = NCH * kb + c
            if i == 0:
                eng.wait_ge(s_mr, 16 * (h + 1))
            wait(eng, s_e, NE * h + i - 1)
            eng.matmul(pb[i % 2], key[v][0:KROWS, kb * P:(kb + 1) * P],
                       qry[v][0:KROWS, c * BANK:(c + 1) * BANK], start=True, stop=True).then_inc(s_b, 1)

        def pe_head(eng, h, v, next_load, first, last):
            a = 0
            w = (v + 1) % ROT
            for kb in range(NBLK):
                for s in range(2):
                    na = (A_PLAN[kb] + 1) // 2 if s == 0 else A_PLAN[kb] // 2
                    if not last:
                        for _ in range(na):
                            if a == 0:
                                eng.wait_ge(s_ld[w], 96 * next_load)
                            a_half(eng, h + 1, w, a)
                            a += 1
                    if s == 0:
                        b_chunk(eng, h, v, kb, 0)
                        b_chunk(eng, h, v, kb, 1)
                        if kb > 0:
                            pv_block(eng, h, kb - 1)
                        elif not first:
                            pv_block(eng, h - 1, NBLK - 1)
                        b_chunk(eng, h, v, kb, 2)
                        b_chunk(eng, h, v, kb, 3)
                if kb == NBLK - 2 and not last:
                    max_transpose(eng, h + 1)
            if last:
                pv_block(eng, h, NBLK - 1)

        block = ctx.enter_context(nc.Block())

        @block.sync
        def _(sp):
            for dst, src in ((wq, wq_t), (wv, wv_t), (wo, wo_t)):
                sp.dma_start(dst[:, :, :], src.rearrange("(k p) n -> p k n", p=P)).then_inc(s_w, 16)
            sp.dma_start(w1[:, :].rearrange("p (k n) -> p k n", k=KC), w1_t.rearrange("(k p) n -> p k n", p=P)).then_inc(s_w, 16)
            sp.dma_start(w2[:, :].rearrange("p (k n) -> p k n", k=KF), w2_t.rearrange("(k p) n -> p k n", p=P)).then_inc(s_w, 16)
            for dst, src in ((idf, ident), (g_col, ln_g), (b_col, ln_b), (bq_col, bq), (b1_col, b1)):
                sp.dma_start(dst[:, :], src).then_inc(s_w, 16)
            for dst, src in ((bv_row, bv), (bo_row, bo), (b2_row, b2)):
                sp.dma_start(dst[:, :], src.to_broadcast((P, C))).then_inc(s_w, 16)

            def store_q(g):
                sp.wait_ge(s_q3, KC * (g + 1))
                for k in range(KC):
                    sp.dma_start(q_dram[:, k * P:(k + 1) * P, ds(g * BANK, BANK)].rearrange("s p n -> p s n"),
                                 qp[:, k, :, :]).then_inc(s_qs, 16)

            sp.dma_start(xin[:, :, :], x_v[0]).then_inc(s_x, 16)
            with sp.Fori(1, NG) as g:
                sp.wait_ge(s_ln, 6 * g)
                sp.wait_ge(s_xb, g)
                sp.dma_start(xin[:, :, :], x_v[ds(g, 1)].rearrange("o p t c -> (o p) t c")).then_inc(s_x, 16)
                store_q(g - 1)
            store_q(NG - 1)

            def load_head(h, v):
                b, hh = h // H, h % H
                src = q_dram[:, ds(hh * D, D), ds(b * L, L)]
                sp.dma_start(key[v][0:3 * D, :], src).then_inc(s_ld[v], 16)
                sp.dma_start(key[v][3 * D:5 * D, :], src[0:2]).then_inc(s_ld[v], 16)
                sp.dma_start(key[v][5 * D:6 * D, :], src[0]).then_inc(s_ld[v], 16)
                at = 0
                for part, times in ((0, 3), (1, 2), (2, 1)):
                    one = src[part:part + 1].to_broadcast((times, D, L)) if times > 1 else src[part]
                    sp.dma_start(qry[v][at * D:(at + times) * D, :], one).then_inc(s_ld[v], 16)
                    at += times

            def max_rows_in(h, v):
                sp.wait_ge(s_mc, h + 1)
                sp.dma_start(qry[v][SPLIT:KROWS, :].rearrange("s (k p) -> s k p", p=P), max_rows[:, :]).then_inc(s_mr, 16)

            def store_o(h):
                sp.wait_ge(s_o, h + 1)
                sp.dma_start(o_dram[ds(h, 1)].rearrange("h c r n -> (h c r) n"), o_sb).then_inc(s_os, 16)

            sp.wait_ge(s_qs, 16 * KC * NG)
            load_head(0, 0)
            load_head(1, 1)
            max_rows_in(0, 0)
            load_head(2, 2)
            max_rows_in(1, 1)

            def sp_head(h, i):
                sp.wait_ge(s_b, NE * h)
                load_head(h + 2, (i + 2) % ROT)
                store_o(h - 1)
                max_rows_in(h + 1, (i + 1) % ROT)
            n_it = (NH - 3) // ROT
            with sp.Fori(0, n_it) as j:
                for u in range(ROT):
                    sp_head(j * ROT + (u + 1), u + 1)
            for h in range(1 + n_it * ROT, NH):
                if h + 2 < NH:
                    sp_head(h, h)
                else:
                    store_o(h - 1)
                    if h + 1 < NH:
                        max_rows_in(h + 1, (h + 1) % ROT)
            store_o(NH - 1)

            sp.wait_ge(s_os, 16 * NH)
            sp.dma_start(sums, o_dram[:, :, D, :].rearrange("h c n -> (h c) n")).then_inc(s_sl, 16)
            sp.wait_ge(s_rc, 1)
            sp.dma_start(r_dram.rearrange("h c n -> (h c) n"), rsum).then_inc(s_rw, 16)
            sp.wait_ge(s_rw, 16)

            def load_o(b):
                for c in range(NCH):
                    g = b * NCH + c
                    wait(sp, s_on, KC * (g - 1))
                    for k in range(KC):
                        h0 = b * H + k * HC
                        sp.dma_start(ot[c % 2][:, k, :], o_dram[ds(h0, HC), c, 0:D, :]).then_inc(s_ol[c % 2], 16)
                        sp.dma_start(rb[c % 2][:, k, :],
                                     r_dram[ds(h0, HC), c:c + 1, :].to_broadcast((HC, D, BANK))).then_inc(s_ol[c % 2], 16)
            load_o(0)
            with sp.Fori(1, NB) as b:
                load_o(b)
            for i in range(2):
                sp.wait_ge(s_out[i], 16 * NG // 2)

        @block.gpsimd
        def _(pool):
            pool.memset(expo[:, :], -0.5).then_inc(s_c, 1)
            pool.memset(eps[:, :], EPS).then_inc(s_c, 1)
            pool.wait_ge(s_w, 16 * N_W)
            pool.tensor_tensor(bias_row[:, :], bo_row[:, :], b2_row[:, :], ALU.add).then_inc(s_c, 1)
            pool.wait_ge(s_c, N_CONST)

            def group(g, first):
                for n in range(2):
                    pool.wait_ge(s_ln, 6 * g + 3 * n + 2)
                    pool.tensor_tensor(veps[:, :], mv[:, :, 1], eps[:, :], ALU.add).then_inc(s_rs, 1)
                    pool.wait_ge(s_rs, 4 * g + 2 * n + 1)
                    pool.tensor_tensor(rstd[:, :], veps[:, :], expo[:, :], ALU.pow).then_inc(s_rs, 1)
                for t in range(TG):
                    last = pool.tensor_tensor(resid[:, ds(g * TG + t, 1), :].rearrange("p o c -> p (o c)"),
                                              xin[:, t, :], bias_row[:, :], ALU.add)
                last.then_inc(s_xb, 1)
                if not first:
                    add_ffn(g - 1)

            def add_ffn(g):
                pool.wait_ge(s_fe, 2 * (g + 1))
                pool.wait_ge(s_xb, g + 1)
                pool.tensor_tensor(resid[:, ds(g * TG, TG), :], resid[:, ds(g * TG, TG), :], f2[:, :, :],
                                   ALU.add).then_inc(s_ra, 1)

            group(0, True)
            with pool.Fori(1, NG) as g:
                group(g, False)

            def stage(h, n):
                b, hh = h // H, h % H
                k0 = n * NBLK // 2
                pool.tensor_copy(vst[:, k0:k0 + NBLK // 2, 0:D],
                                 v_all[:, ds(b * NBLK + k0, NBLK // 2), ds(hh * D, D)]).then_inc(s_vs, 1)
            pool.wait_ge(s_vd, TG * NG)
            stage(0, 0)
            stage(0, 1)
            add_ffn(NG - 1)
            with pool.Fori(1, NH) as h:
                for n in range(2):
                    pool.wait_ge(s_pv, NBLK * h - NBLK // 2 * (1 - n))
                    stage(h, n)

        @block.vector
        def _(dve):
            dve.memset(ones[:, :], 1.0).then_inc(s_c, 1)
            dve.memset(vst[:, :, :], 1.0).then_inc(s_c, 1)
            for i in range(ROT):
                dve.memset(key[i][SPLIT:P, :], 1.0).then_inc(s_c, 1)
            dve.wait_ge(s_w, 16 * N_W)
            dve.tensor_copy(idb[:, :], idf[:, :]).then_inc(s_c, 1)
            dve.tensor_reduce(wabs[:, 0:1], w1[:, :], AX.X, ALU.add, apply_absolute_value=True)
            dve.tensor_reduce(wabs[:, 1:2], w2[:, :], AX.X, ALU.add, apply_absolute_value=True).then_inc(s_wd, 1)
            dve.wait_ge(s_wp, 1)
            dve.tensor_scalar(thr[:, :], bank(7)[:, 0:2], 1.0 / (FF * C), 1e-8, ALU.mult, ALU.max).then_inc(s_wd, 1)
            dve.wait_ge(s_wd, 2)
            dve.tensor_scalar(half[:, :], thr[:, :], 0.5, None, ALU.mult)
            dve.tensor_scalar(nhalf[:, :], thr[:, :], -0.5, None, ALU.mult).then_inc(s_wd, 1)
            dve.wait_ge(s_wd, 3)
            n = 3
            for j, (src, dst) in enumerate(((w1, w1t), (w2, w2t))):
                dve.tensor_scalar(below, src[:, :], nhalf[:, j:j + 1], None, ALU.is_lt).then_inc(s_wd, 1)
                n += 1
                dve.wait_ge(s_wd, n)
                dve.scalar_tensor_tensor(out=dst[:, :, :].rearrange("p k n -> p (k n)"), in0=src[:, :],
                                         scalar=half[:, j:j + 1], in1=below, op0=ALU.is_gt,
                                         op1=ALU.subtract).then_inc(s_wd, 1)
                n += 1
                dve.wait_ge(s_wd, n)

            def norm(g, n, src, dst):
                base = 6 * g + 3 * n
                for t in range(TG):
                    last = dve.bn_stats(stats[:, t, :], src[:, t, :])
                last.then_inc(s_ln, 1)
                dve.wait_ge(s_ln, base + 1)
                dve.memset(carrier[:, :], 0.0)
                for t in range(TG):
                    last = dve.bn_aggr(mv[:, t, :], stats[:, t, :])
                last.then_inc(s_ln, 1)
                dve.wait_ge(s_ln, base + 2)
                dve.wait_ge(s_rs, 4 * g + 2 * n + 2)
                for t in range(TG):
                    last = dve.tensor_scalar(dst[:, t, :], src[:, t, :], mv[:, t, 0:1], rstd[:, t:t + 1],
                                             ALU.subtract, ALU.mult)
                last.then_inc(s_ln, 1)
                dve.wait_ge(s_ln, base + 3)

            def group(g, first):
                dve.wait_ge(s_x, 16 * (g + 1))
                if not first:
                    dve.wait_ge(s_tr, g)
                norm(g, 0, xin, xn)
                norm(g, 1, xn, zn)
                dve.wait_ge(s_tr, g + 1)
                if not first:
                    dve.wait_ge(s_x2, KC * g)
                for k in range(KC):
                    dve.wait_ge(s_x1, KC * g + k + 1)
                    dve.tensor_tensor(xr[:, k, :], tr_x[k], x1[:, k, :], ALU.subtract).then_inc(s_xr, 1)
                if not first:
                    dve.wait_ge(s_v, 2 * g)
                for k in range(KC):
                    dve.tensor_scalar(zt[:, k, :], tr_z[k], g_col[:, k:k + 1], b_col[:, k:k + 1],
                                      ALU.mult, ALU.add).then_inc(s_z, 1)
                for k in range(KC):
                    dve.wait_ge(s_x2, KC * g + k + 1)
                    dve.tensor_tensor(x3[:, k, :], xr[:, k, :], x2[:, k, :], ALU.subtract).then_inc(s_x3, 1)
                if not first:
                    dve.wait_ge(s_qs, 16 * KC * g)
                for k in range(KC):
                    dve.wait_ge(s_qa, 2 * (KC * g + k + 1))
                    dve.tensor_tensor(qr[:, k, :], qf[:, k, :], qp[:, k, 0, :], ALU.subtract).then_inc(s_qr, 1)
                for k in range(KC):
                    dve.wait_ge(s_q2, KC * g + k + 1)
                    dve.tensor_tensor(qp[:, k, 2, :], qr[:, k, :], qp[:, k, 1, :], ALU.subtract).then_inc(s_q3, 1)
                for t in range(TG):
                    dve.wait_ge(s_v, 2 * g + t // 2 + 1)
                    dve.tensor_tensor(v_all[:, ds(g * TG + t, 1), :].rearrange("p o c -> p (o c)"),
                                      pq[t // 2][:, (t % 2) * C:(t % 2 + 1) * C], bv_row[:, :], ALU.add).then_inc(s_vd, 1)

            group(0, True)
            with dve.Fori(1, NG) as g:
                group(g, False)

            def row_max(h):
                for a in range(NHALF):
                    dve.wait_ge(s_a, NHALF * h + a + 1)
                    dve.tensor_reduce(part_max[:, a // 2, a % 2:a % 2 + 1], pa[a % 2], AX.X, ALU.max).then_inc(s_r, 1)
                dve.wait_ge(s_r, NHALF * (h + 1))
                dve.tensor_reduce(neg_max[:, :], part_max[:, :, :], AX.X, ALU.max, negate=True).then_inc(s_m, 1)
                dve.wait_ge(s_m, 3 * h + 1)
                dve.tensor_copy(max_split[:, 0, :], neg_max[:, :]).then_inc(s_m, 1)
                dve.wait_ge(s_m, 3 * h + 2)
                dve.tensor_tensor(max_split[:, 1, :], neg_max[:, :], max_split[:, 0, :], ALU.subtract).then_inc(s_m, 1)
                dve.wait_ge(s_mt, h + 1)
                if not (isinstance(h, int) and h == 0):
                    dve.wait_ge(s_mr, 16 * h)
                dve.tensor_copy(max_rows[:, :], pm[0:2 * NBLK, 0:P]).then_inc(s_mc, 1)
            row_max(0)
            with dve.Fori(1, NH) as h:
                row_max(h)

            dve.wait_ge(s_sl, 16)
            dve.reciprocal(rsum, sums).then_inc(s_rc, 1)

            def add_resid(g, i, stored):
                wait(dve, s_out[i], 16 * stored)
                for t in range(0, TG, 2):
                    dve.wait_ge(s_y, 2 * g + t // 2 + 1)
                    dve.tensor_tensor(y[i][:, t:t + 2, :], py[t // 2].rearrange("p (t c) -> p t c", t=2),
                                      resid[:, ds(g * TG + t, 2), :], ALU.add).then_inc(s_yd, 1)

            def normalise(b, first):
                for c in range(NCH):
                    g = b * NCH + c
                    dve.wait_ge(s_ol[c % 2], 32 * KC * (b * NCH // 2 + c // 2 + 1))
                    wait(dve, s_y, 2 * (g - 1))
                    for k in range(KC):
                        dve.tensor_tensor(on[c % 2][:, k, :], ot[c % 2][:, k, :], rb[c % 2][:, k, :],
                                          ALU.mult).then_inc(s_on, 1)
                    if c > 0 or not first:
                        add_resid(g - 1, (c - 1) % 2, b * (NCH // 2) + (c - 1) // 2)
            normalise(0, True)
            with dve.Fori(1, NB) as b:
                normalise(b, False)
            add_resid(NG - 1, (NG - 1) % 2, (NG - 1) // 2)

        @block.scalar
        def _(act):
            act.wait_ge(s_w, 16 * N_W)

            def group(g, first):
                act.wait_ge(s_tr, g + 1)
                if not first:
                    act.wait_ge(s_h, KF * g)
                for k in range(KC):
                    act.activation(x1[:, k, :], tr_x[k], ACT.Copy).then_inc(s_x1, 1)
                for k in range(KC):
                    act.wait_ge(s_xr, KC * g + k + 1)
                    act.activation(x2[:, k, :], xr[:, k, :], ACT.Copy).then_inc(s_x2, 1)
                if not first:
                    ffn_out(g - 1)
                    act.wait_ge(s_q3, KC * g)
                    act.wait_ge(s_qs, 16 * KC * g)
                for k in range(KC):
                    act.wait_ge(s_q, KC * g + k + 1)
                    act.activation(qf[:, k, :], pq[k], ACT.Identity, bias=bq_col[:, k:k + 1]).then_inc(s_qa, 1)
                    act.activation(qp[:, k, 0, :], pq[k], ACT.Identity, bias=bq_col[:, k:k + 1]).then_inc(s_qa, 1)
                for k in range(KC):
                    act.wait_ge(s_qr, KC * g + k + 1)
                    act.activation(qp[:, k, 1, :], qr[:, k, :], ACT.Copy).then_inc(s_q2, 1)
                for f in range(KF):
                    act.wait_ge(s_h, KF * g + f + 1)
                    act.activation(hid[:, f, :], pf[f % 2], ACT.Gelu, bias=b1_col[:, f:f + 1]).then_inc(s_g, 1)

            def ffn_out(g):
                for j in range(2):
                    act.wait_ge(s_f, 2 * g + j + 1)
                    if j == 0:
                        wait(act, s_ra, g)
                    act.activation(f2[:, 2 * j:2 * j + 2, :].rearrange("p t c -> p (t c)"), pq[j],
                                   ACT.Copy).then_inc(s_fe, 1)

            group(0, True)
            with act.Fori(1, NG) as g:
                group(g, False)
            ffn_out(NG - 1)

            def evacuate(h):
                act.wait_ge(s_pv, NBLK * (h + 1))
                wait(act, s_os, 16 * h)
                act.activation(o_sb, pv, ACT.Copy).then_inc(s_o, 1)

            def head(h, first):
                for kb in range(NBLK):
                    for c in range(NCH):
                        act.wait_ge(s_b, NE * h + NCH * kb + c + 1)
                        if c == 0 and not (first and kb < 2):
                            act.wait_ge(s_pv, NBLK * h + kb - 1)
                        act.activation(prob[kb % 2][:, c * BANK:(c + 1) * BANK], pb[c % 2], ACT.Exp,
                                       scale=SCALE).then_inc(s_e, 1)
                        if kb == 0 and c == 1 and not first:
                            evacuate(h - 1)
            head(0, True)
            with act.Fori(1, NH) as h:
                head(h, False)
            evacuate(NH - 1)

            with act.Fori(0, NB) as b:
                for c in range(NCH):
                    g = b * NCH + c
                    act.wait_ge(s_yd, 2 * (g + 1))
                    act.dma_start(out_v[ds(g, 1)].rearrange("o p t c -> (o p) t c"), y[c % 2]).then_inc(s_out[c % 2], 16)

        @block.tensor
        def _(pe):
            pe.wait_ge(s_w, 16 * N_W)
            pe.wait_ge(s_c, N_CONST)
            pe.wait_ge(s_wd, 1)
            pe.matmul(bank(7)[:, 0:2], ones[:, :], wabs[:, :], start=True, stop=True).then_inc(s_wp, 1)
            pe.wait_ge(s_wd, 7)

            def ffn_down(g, t):
                if t == 0:
                    pe.wait_ge(s_g, KF * (g + 1))
                    pe.wait_ge(s_vd, TG * (g + 1))
                for f in range(KF):
                    mm = pe.matmul(pq[t // 2][:, (t % 2) * C:(t % 2 + 1) * C], hid[:, f, t * P:(t + 1) * P],
                                   w2t[:, f, :], start=(f == 0), stop=(f == KF - 1))
                if t % 2:
                    mm.then_inc(s_f, 1)

            def group(g, first):
                pe.wait_ge(s_ln, 6 * g + 6)
                if not first:
                    pe.wait_ge(s_z, KC * g)
                    pe.wait_ge(s_xr, KC * g)
                for src, dst in ((xn, tr_x), (zn, tr_z)):
                    for k in range(KC):
                        for t in range(TG):
                            mm = pe.transpose(dst[k][:, t * P:(t + 1) * P], src[:, t, k * P:(k + 1) * P], idf[:, :])
                mm.then_inc(s_tr, 1)
                if not first:
                    for t in range(TG):
                        ffn_down(g - 1, t)
                    pe.wait_ge(s_fe, 2 * g)
                for o in range(KC):
                    for k in range(KC):
                        if o == 0:
                            pe.wait_ge(s_z, KC * g + k + 1)
                        mm = pe.matmul(pq[o], wq[:, k, o * P:(o + 1) * P], zt[:, k, :], start=(k == 0), stop=(k == KC - 1))
                    mm.then_inc(s_q, 1)

                def hidden(f):
                    if f >= 2 or not first:
                        pe.wait_ge(s_g, KF * g + f - 1)
                    for k in range(KC):
                        for i, part in enumerate((x1, x2, x3)):
                            mm = pe.matmul(pf[f % 2], w1t[:, k, f * P:(f + 1) * P], part[:, k, :],
                                           start=(k == 0 and i == 0), stop=(k == KC - 1 and i == 2))
                    mm.then_inc(s_h, 1)
                pe.wait_ge(s_x3, KC * (g + 1))
                hidden(0)
                hidden(1)
                pe.wait_ge(s_qa, 2 * KC * (g + 1))
                for t in range(TG):
                    for k in range(KC):
                        mm = pe.matmul(pq[t // 2][:, (t % 2) * C:(t % 2 + 1) * C], zt[:, k, t * P:(t + 1) * P],
                                       wv[:, k, :], start=(k == 0), stop=(k == KC - 1))
                    if t % 2:
                        mm.then_inc(s_v, 1)
                for f in range(2, KF):
                    hidden(f)

            group(0, True)
            with pe.Fori(1, NG) as g:
                group(g, False)

            pe.wait_ge(s_z, KC * NG)
            pe.wait_ge(s_xr, KC * NG)
            for t in range(TG):
                ffn_down(NG - 1, t)
            pe.wait_ge(s_ld[0], 96)
            for a in range(NHALF):
                a_half(pe, 0, 0, a)
            max_transpose(pe, 0)
            pe.wait_ge(s_fe, 2 * NG)
            pe_head(pe, 0, 0, 1, True, False)
            with pe.Fori(0, (NH - 2) // ROT) as j:
                for u in range(ROT):
                    pe_head(pe, j * ROT + (u + 1), (u + 1) % ROT, j + (u + 2) // ROT + 1, False, False)
            pe_head(pe, NH - 1, (NH - 1) % ROT, None, False, True)

            def project(b):
                for c in range(NCH):
                    g = b * NCH + c
                    pe.wait_ge(s_on, KC * (g + 1))
                    for t in range(TG):
                        if t % 2 == 0:
                            wait(pe, s_yd, 2 * g + t // 2 - 1)
                        for k in range(KC):
                            mm = pe.matmul(py[t // 2][:, (t % 2) * C:(t % 2 + 1) * C], on[c % 2][:, k, t * P:(t + 1) * P],
                                           wo[:, k, :], start=(k == 0), stop=(k == KC - 1))
                        if t % 2:
                            mm.then_inc(s_y, 1)
            project(0)
            with pe.Fori(1, NB) as b:
                project(b)


def kernel(L0_attn_x, L0_attn_ln1_g, L0_attn_ln1_b, L0_attn_w_in, L0_attn_b_in, L0_attn_w_out, L0_attn_b_out,
           L0_ffn_W1, L0_ffn_b1, L0_ffn_W2, L0_ffn_b2):
    import numpy as np
    import concourse.bacc as bacc
    from concourse.bass_utils import run_bass_kernel_spmd

    c = L0_attn_x.shape[2]

    def array(a):
        return np.ascontiguousarray(np.asarray(a))

    def columns(v):
        return array(np.asarray(v).reshape(-1, P).T)

    w_in, b_in = np.asarray(L0_attn_w_in), np.asarray(L0_attn_b_in)
    arrays = {
        "x": array(L0_attn_x),
        "ln_g": columns(L0_attn_ln1_g), "ln_b": columns(L0_attn_ln1_b),
        "wq_t": array(w_in[0:c].T), "wv_t": array(w_in[2 * c:3 * c].T), "wo_t": array(np.asarray(L0_attn_w_out).T),
        "bq": columns(b_in[0:c]), "bv": array(b_in[None, 2 * c:3 * c]), "bo": array(np.asarray(L0_attn_b_out)[None, :]),
        "w1_t": array(np.asarray(L0_ffn_W1).T), "b1": columns(L0_ffn_b1),
        "w2_t": array(np.asarray(L0_ffn_W2).T), "b2": array(np.asarray(L0_ffn_b2)[None, :]),
        "ident": np.eye(P, dtype=np.float32),
    }
    nc = bacc.Bacc("TRN2", target_bir_lowering=False, num_devices=1)
    args = [nc.dram_tensor(f"in_{n}", a.shape, mybir.dt.from_np(a.dtype), kind="ExternalInput").ap()
            for n, a in arrays.items()]
    out = nc.dram_tensor("out", tuple(L0_attn_x.shape), F32, kind="ExternalOutput").ap()
    attention_ffn(nc, *args, out)
    r = run_bass_kernel_spmd(nc, [{f"in_{n}": a for n, a in arrays.items()}], core_ids=[0])
    return r.results[0]["out"]
```

```python
from contextlib import ExitStack

import concourse.bass as bass
from concourse import mybir

F32 = mybir.dt.float32
BF16 = mybir.dt.bfloat16
ALU = mybir.AluOpType
ACT = mybir.ActivationFunctionType
AX = mybir.AxisListType
ds = bass.ds

P = 128
EPS = 1e-5
BANK = 512

KEY_PARTS = (0, 1, 2, 0, 1, 0)
QRY_PARTS = (0, 0, 0, 1, 1, 2)
AHEAD = 2
ROT = 3


def wait(eng, sem, value):
    if not isinstance(value, int) or value > 0:
        eng.wait_ge(sem, value)


def attention_ffn(nc, x, ln_g, ln_b, wq_t, wv_t, wo_t, bq, bv, bo, w1_t, b1, w2_t, b2, ident, out):
    NB, L, C = x.shape
    FF = w1_t.shape[1]
    D = 16
    H = C // D
    NH = NB * H
    KC = C // P
    KF = FF // P
    NBLK = L // P
    NCH = L // BANK
    TG = BANK // P
    NT = NB * L // P
    NG = NT // TG
    GB = NG // NB
    HC = P // D
    NHALF = 2 * NBLK
    NE = NBLK * NCH
    SPLIT = len(KEY_PARTS) * D
    KROWS = SPLIT + 2
    W = 2 * BANK
    SCALE = 1.0 / float(D) ** 0.5
    assert NCH == 4 and NB == 2 and NH > 2 * ROT

    x_v = x.rearrange("b (g t p) c -> (b g) p t c", t=TG, p=P)
    out_v = out.rearrange("b (g t p) c -> (b g) p t c", t=TG, p=P)
    q_dram = nc.dram_tensor("q_parts", (3, C, NB * L), BF16, kind="Internal").ap()
    o_dram = nc.dram_tensor("o_heads", (NH, NCH, 2 * D, BANK), F32, kind="Internal").ap()
    r_dram = nc.dram_tensor("o_recip", (NH, NCH, BANK), F32, kind="Internal").ap()

    ctx = ExitStack()
    with ctx:
        def sb(name, shape, dt=F32):
            return ctx.enter_context(nc.sbuf_tensor(name, shape, dt))

        def sem(name):
            return ctx.enter_context(nc.semaphore(name))

        wq = sb("wq", [P, KC, C]); wv = sb("wv", [P, KC, C]); wo = sb("wo", [P, KC, C])
        w1 = sb("w1", [P, KC * FF]); w2 = sb("w2", [P, KF * C])
        w1t = sb("w1_ternary", [P, KC, FF], BF16)
        w2t = sb("w2_ternary", [P, KF, C], BF16)
        idf = sb("ident_f32", [P, P]); idb = sb("ident_bf16", [P, P], BF16)
        ones = sb("ones", [P, P])
        g_col = sb("g_col", [P, KC]); b_col = sb("b_col", [P, KC])
        bq_col = sb("bq_col", [P, KC]); b1_col = sb("b1_col", [P, KF])
        bv_row = sb("bv_row", [P, C]); bo_row = sb("bo_row", [P, C]); b2_row = sb("b2_row", [P, C])
        bias_row = sb("bias_row", [P, C])
        wabs = sb("wabs", [P, 2]); thr = sb("thr", [P, 2]); half = sb("half", [P, 2]); nhalf = sb("nhalf", [P, 2])
        expo = sb("minus_half", [P, TG])
        xin = sb("xin", [P, TG, C]); xn = sb("xn", [P, TG, C]); zn = sb("zn", [P, TG, C])
        stats = sb("stats", [P, TG, 6]); mv = sb("mean_var", [P, TG, 2])
        carrier = sb("wait_carrier", [P, 1])
        eps = sb("eps", [P, TG])
        veps = sb("var_eps", [P, TG]); rstd = sb("rstd", [P, TG])
        x1 = sb("x1", [P, KC, BANK], BF16); x2 = sb("x2", [P, KC, BANK], BF16); x3 = sb("x3", [P, KC, BANK], BF16)
        xr = sb("x_rest", [P, KC, BANK])
        zt = sb("zt", [P, KC, BANK])
        qf = sb("qf", [P, KC, BANK]); qr = sb("q_rest", [P, KC, BANK])
        qp = sb("q_split", [P, KC, 3, BANK], BF16)
        hid = sb("hidden", [P, KF, BANK])
        hid3 = sb("hidden3", [P, KF, BANK], BF16)
        hp = [w1[:, :].bitcast(BF16).rearrange("p (f n) -> p f n", f=KF),
              w2[:, :].bitcast(BF16).rearrange("p (f n) -> p f n", f=KF), hid3]
        below = hid3[:, :, :].rearrange("p f n -> p (f n)").bitcast(F32)
        f2 = sb("ffn_out", [P, TG, C])
        resid = sb("resid", [P, NT, C])
        v_all = sb("v_all", [P, NT, C])
        key = [sb(f"key{i}", [P, L], BF16) for i in range(ROT)]
        qry = [sb(f"qry{i}", [P, L], BF16) for i in range(ROT)]
        vst = sb("v_ones", [P, NBLK, 2 * D])
        prob = [w1, w2]
        part_max = sb("part_max", [P, NBLK, 2]); neg_max = sb("neg_max", [P, NBLK])
        max_split = sb("max_split", [P, 2, NBLK], BF16)
        max_rows = sb("max_rows", [2 * NBLK, P], BF16)
        o_sb = xin[:, 0:2, :].rearrange("p t c -> p (t c)")
        sums, rsum = ([z[0:H * NCH, 2 * b:2 * b + 2, :].rearrange("p t c -> p (t c)") for b in range(NB)]
                      for z in (xn, zn))
        ot = [hid[:, KC * i:KC * (i + 1), :] for i in range(2)]
        rb = [hid[:, KC * (i + 2):KC * (i + 3), :] for i in range(2)]
        on = [xr, qf]
        y = [z[:, :, :].rearrange("p k (t c) -> p (k t) c", c=C) for z in (zt, qr)]

        ps = ctx.enter_context(nc.psum_tensor("ps", [P, 8 * BANK], F32))

        def bank(b, n=1):
            return ps[:, b * BANK:(b + n) * BANK]
        tr_x = [bank(0), bank(1)]
        tr_z = [bank(2), bank(3)]
        pq = [bank(4), bank(5)]
        pf = [bank(6), bank(7)]
        pa = [bank(0, 2), bank(2, 2)]
        pb = [bank(4), bank(5), bank(7)]
        pb_last = pb + [bank(0), bank(1)]
        pm = pb[0][:, 0:P // 2].bitcast(BF16)
        pv = bank(6)
        py = [bank(0), bank(1)]

        s_id = sem("ident_loaded"); s_col = sem("columns_loaded"); s_row = sem("rows_loaded")
        s_wq = sem("wq_loaded"); s_wv = sem("wv_loaded"); s_wo = sem("wo_loaded")
        s_w = [sem("w1_loaded"), sem("w2_loaded")]
        s_c = sem("ones_done"); s_pc = sem("pool_constants"); s_x = sem("x_loaded"); s_idb = sem("ident_bf16_done")
        s_wa = sem("weight_abs_sums"); s_wp = sem("weight_scales"); s_wd = sem("weight_dve")
        s_ln = sem("ln_dve"); s_rs = sem("ln_pool"); s_xb = sem("x_plus_bias")
        s_tr = sem("transposed"); s_x1 = sem("x1"); s_xr = sem("x_rest_done"); s_x2 = sem("x2"); s_x3 = sem("x3")
        s_z = sem("zt_done"); s_q = sem("q_psum"); s_qa = sem("q_biased"); s_qr = sem("q_rest_done")
        s_q2 = sem("q2"); s_q3 = sem("q3"); s_qs = sem("q_stored"); s_v = sem("v_psum"); s_vd = sem("v_done")
        s_h = sem("hidden_psum"); s_g = sem("gelu_done"); s_hr = sem("hidden_rest"); s_h2 = [sem("hidden2_even"), sem("hidden2_odd")]; s_h3 = sem("hidden3_done");
        s_f = sem("ffn_psum"); s_fe = sem("ffn_evacuated")
        s_ra = sem("resid_done")
        s_ld = [sem(f"head_loaded{i}") for i in range(ROT)]; s_a = sem("pass_a"); s_r = sem("row_max"); s_m = sem("max_dve")
        s_mt = sem("max_transposed"); s_mc = sem("max_copied"); s_mr = sem("max_rows_in_place")
        s_b = sem("pass_b"); s_e = sem("exp_done"); s_vs = sem("v_staged"); s_pv = sem("pv_done")
        s_o = sem("o_evacuated"); s_os = sem("o_stored")
        s_sl = sem("sums_loaded"); s_rc = sem("recip_done"); s_rw = sem("recip_stored")
        s_ol = [sem(f"o_loaded{i}") for i in range(2)]; s_on = sem("o_normalised"); s_y = sem("y_psum"); s_yd = sem("y_done")
        s_out = [sem(f"out_stored{i}") for i in range(2)]

        def a_half(eng, h, v, a):
            n = a % 2
            wait(eng, s_r, NHALF * h + a - 1)
            blk, half_ = a // 2, a % 2
            for j in range(2):
                col = half_ * W + j * BANK
                mm = eng.matmul(pa[n][:, j * BANK:(j + 1) * BANK], key[v][0:SPLIT, blk * P:(blk + 1) * P],
                                qry[v][0:SPLIT, col:col + BANK], start=True, stop=True)
            mm.then_inc(s_a, 1)

        MAX_AT = NCH * (NBLK - AHEAD + 1)
        assert (NE + 2) % len(pb) == 0 and MAX_AT % len(pb) == 0

        def turn(i):
            return i if i < MAX_AT else i + 2

        def ring_bank(i, last):
            return pb_last[i % len(pb_last)] if last else pb[turn(i) % len(pb)]

        def max_transpose(eng, h):
            eng.wait_ge(s_m, 3 * h + 3)
            wait(eng, s_e, NE * (h - 1) + MAX_AT - len(pb) + 1)
            eng.transpose(pm[0:2 * NBLK, 0:P], max_split[:, :, :].rearrange("p s k -> p (s k)"), idb[:, :]).then_inc(s_mt, 1)

        def pv_block(eng, h, kb):
            eng.wait_ge(s_e, NE * h + NCH * (kb + 1))
            if kb % (NBLK // 2) == 0:
                eng.wait_ge(s_vs, 2 * h + 1 + kb // (NBLK // 2))
            if kb == 0:
                wait(eng, s_o, h)
            for c in range(NCH):
                mm = eng.matmul(pv[32 * c:32 * c + 2 * D, :], vst[:, kb, :],
                                prob[kb % 2][:, c * BANK:(c + 1) * BANK],
                                start=(kb == 0), stop=(kb == NBLK - 1))
            mm.then_inc(s_pv, 1)

        def b_chunk(eng, h, v, kb, c, last):
            i = NCH * kb + c
            if i == 0:
                eng.wait_ge(s_mr, 16 * (h + 1))
            before = turn(i) - len(pb)
            if last and i >= len(pb):
                if i >= len(pb_last):
                    eng.wait_ge(s_e, NE * h + i - len(pb_last) + 1)
            elif before == MAX_AT:
                eng.wait_ge(s_mc, h + 2)
            elif before < MAX_AT:
                wait(eng, s_e, NE * h + before + 1)
            elif before == MAX_AT + 1:
                eng.wait_ge(s_e, NE * h + before - len(pb) + 1)
            else:
                eng.wait_ge(s_e, NE * h + before - 1)
            eng.matmul(ring_bank(i, last), key[v][0:KROWS, kb * P:(kb + 1) * P],
                       qry[v][0:KROWS, c * BANK:(c + 1) * BANK], start=True, stop=True).then_inc(s_b, 1)

        def pe_head(eng, j, k):
            h = j * ROT + k
            first, left = isinstance(h, int) and h == 0, NH - 1 - h if isinstance(h, int) else ROT
            last = left == 0
            if last:
                eng.wait_ge(s_r, NHALF * NH)
            for kb in range(NBLK):
                b_chunk(eng, h, k % ROT, kb, 0, last)
                b_chunk(eng, h, k % ROT, kb, 1, last)
                if kb > 0:
                    pv_block(eng, h, kb - 1)
                elif not first:
                    pv_block(eng, h - 1, NBLK - 1)
                b_chunk(eng, h, k % ROT, kb, 2, last)
                b_chunk(eng, h, k % ROT, kb, 3, last)
                ahead = 1 + (kb + AHEAD) // NBLK
                if left >= ahead:
                    blk = (kb + AHEAD) % NBLK
                    if blk == 0:
                        eng.wait_ge(s_ld[(k + ahead) % ROT], 96 * (j + (k + ahead) // ROT + 1))
                    a_half(eng, h + ahead, (k + ahead) % ROT, 2 * blk)
                    a_half(eng, h + ahead, (k + ahead) % ROT, 2 * blk + 1)
                if kb == NBLK - AHEAD and left >= 1:
                    max_transpose(eng, h + 1)
            if left == 0:
                pv_block(eng, h, NBLK - 1)

        block = ctx.enter_context(nc.Block())

        @block.sync
        def _(sp):
            sp.dma_start(xin[:, :, :], x_v[0]).then_inc(s_x, 16)
            for dst, src, s in ((wq, wq_t, s_wq), (w2, w2_t, s_w[1]), (wv, wv_t, s_wv), (wo, wo_t, s_wo)):
                if dst is w2:
                    dst = w2[:, :].rearrange("p (k n) -> p k n", k=KF)
                sp.dma_start(dst[:, :, :], src.rearrange("(k p) n -> p k n", p=P)).then_inc(s, 16)

            def store_q(g):
                sp.wait_ge(s_q3, KC * (g + 1))
                for k in range(KC):
                    sp.dma_start(q_dram[:, k * P:(k + 1) * P, ds(g * BANK, BANK)].rearrange("s p n -> p s n"),
                                 qp[:, k, :, :]).then_inc(s_qs, 16)

            with sp.Fori(1, NG) as g:
                sp.wait_ge(s_ln, 6 * g)
                sp.wait_ge(s_xb, g)
                sp.dma_start(xin[:, :, :], x_v[ds(g, 1)].rearrange("o p t c -> (o p) t c")).then_inc(s_x, 16)
                store_q(g - 1)
            def load_head(h, v):
                b, hh = h // H, h % H
                src = q_dram[:, ds(hh * D, D), ds(b * L, L)]
                sp.dma_start(key[v][0:3 * D, :], src).then_inc(s_ld[v], 16)
                sp.dma_start(key[v][3 * D:5 * D, :], src[0:2]).then_inc(s_ld[v], 16)
                sp.dma_start(key[v][5 * D:6 * D, :], src[0]).then_inc(s_ld[v], 16)
                at = 0
                for part, times in ((0, 3), (1, 2), (2, 1)):
                    one = src[part:part + 1].to_broadcast((times, D, L)) if times > 1 else src[part]
                    sp.dma_start(qry[v][at * D:(at + times) * D, :], one).then_inc(s_ld[v], 16)
                    at += times

            def max_rows_in(h, v):
                sp.wait_ge(s_mc, h + 1)
                sp.dma_start(qry[v][SPLIT:KROWS, :].rearrange("s (k p) -> s k p", p=P), max_rows[:, :]).then_inc(s_mr, 16)

            def store_o(h):
                sp.wait_ge(s_o, h + 1)
                sp.dma_start(o_dram[ds(h, 1)].rearrange("h c r n -> (h c r) n"), o_sb).then_inc(s_os, 16)

            load_head(0, 0)
            load_head(1, 1)
            store_q(NG - 1)
            sp.wait_ge(s_qs, 16 * KC * NG)
            max_rows_in(0, 0)
            load_head(2, 2)
            max_rows_in(1, 1)

            def sp_head(h, i):
                sp.wait_ge(s_b, NE * h)
                load_head(h + 2, (i + 2) % ROT)
                store_o(h - 1)
                max_rows_in(h + 1, (i + 1) % ROT)
            n_it = (NH - 3) // ROT
            with sp.Fori(0, n_it) as j:
                for u in range(ROT):
                    sp_head(j * ROT + (u + 1), u + 1)
            for h in range(1 + n_it * ROT, NH):
                if h + 2 < NH:
                    sp_head(h, h)
                else:
                    store_o(h - 1)
                    if h + 1 < NH:
                        max_rows_in(h + 1, (h + 1) % ROT)

            def spread_recip(b):
                sp.dma_start(sums[b], o_dram[b * H:(b + 1) * H, :, D, :].rearrange("h c n -> (h c) n")).then_inc(s_sl, 16)
                sp.wait_ge(s_rc, b + 1)
                sp.dma_start(r_dram[b * H:(b + 1) * H].rearrange("h c n -> (h c) n"), rsum[b]).then_inc(s_rw, 16)
                sp.wait_ge(s_rw, 16 * (b + 1))

            def load_o(b):
                for c in range(NCH):
                    g = b * NCH + c
                    wait(sp, s_on, KC * (g - 1))
                    for k in range(KC):
                        h0 = b * H + k * HC
                        sp.dma_start(ot[c % 2][:, k, :], o_dram[ds(h0, HC), c, 0:D, :]).then_inc(s_ol[c % 2], 16)
                        sp.dma_start(rb[c % 2][:, k, :],
                                     r_dram[ds(h0, HC), c:c + 1, :].to_broadcast((HC, D, BANK))).then_inc(s_ol[c % 2], 16)
            sp.wait_ge(s_os, 16 * (NH - 1))
            spread_recip(0)
            load_o(0)
            store_o(NH - 1)
            sp.wait_ge(s_os, 16 * NH)
            spread_recip(1)
            load_o(1)
            for i in range(2):
                sp.wait_ge(s_out[i], 16 * NG // 2)

        @block.gpsimd
        def _(pool):
            sets = [(expo[:, :], -0.5), (eps[:, :], EPS), (vst[:, :, :], 1.0)] + [(k[SPLIT:P, :], 1.0) for k in key]

            def constants(n0, n1):
                for n in range(n0, n1):
                    dst, value = sets[n]
                    pool.memset(dst, value).then_inc(s_pc, 1)
                    pool.wait_ge(s_pc, n + 1)

            def rsqrt(g):
                for n in range(2):
                    pool.wait_ge(s_ln, 6 * g + 3 * n + 2)
                    pool.tensor_tensor(veps[:, :], mv[:, :, 1], eps[:, :], ALU.add).then_inc(s_rs, 1)
                    pool.wait_ge(s_rs, 4 * g + 2 * n + 1)
                    pool.tensor_tensor(rstd[:, :], veps[:, :], expo[:, :], ALU.pow).then_inc(s_rs, 1)

            def group(g, add=True):
                rsqrt(g)
                residual(g, add)

            def residual(g, add=True):
                for t in range(TG):
                    last = pool.tensor_tensor(resid[:, ds(g * TG + t, 1), :].rearrange("p o c -> p (o c)"),
                                              xin[:, t, :], bias_row[:, :], ALU.add)
                last.then_inc(s_xb, 1)
                if add:
                    add_ffn(g - 2)

            def add_ffn(g):
                pool.wait_ge(s_fe, 2 * (g + 1))
                pool.wait_ge(s_xb, g + 1)
                pool.tensor_tensor(resid[:, ds(g * TG, TG), :], resid[:, ds(g * TG, TG), :], f2[:, :, :],
                                   ALU.add).then_inc(s_ra, 1)

            constants(0, 2)
            rsqrt(0)
            pool.wait_ge(s_row, 48)
            pool.tensor_tensor(bias_row[:, :], bo_row[:, :], b2_row[:, :], ALU.add).then_inc(s_row, 1)
            pool.wait_ge(s_row, 49)
            residual(0, add=False)
            group(1, add=False)
            constants(2, len(sets))
            with pool.Fori(2, NG) as g:
                group(g)

            def stage(h, n):
                b, hh = h // H, h % H
                k0 = n * NBLK // 2
                pool.tensor_copy(vst[:, k0:k0 + NBLK // 2, 0:D],
                                 v_all[:, ds(b * NBLK + k0, NBLK // 2), ds(hh * D, D)]).then_inc(s_vs, 1)
            pool.wait_ge(s_vd, TG * NG)
            stage(0, 0)
            stage(0, 1)
            add_ffn(NG - 2)
            add_ffn(NG - 1)
            with pool.Fori(1, NH) as h:
                for n in range(2):
                    pool.wait_ge(s_pv, NBLK * h - NBLK // 2 * (1 - n))
                    stage(h, n)

        @block.vector
        def _(dve):
            dve.memset(ones[:, :], 1.0).then_inc(s_c, 1)

            def ternary(j, src, dst):
                n = 4 * j
                dve.wait_ge(s_wp, j + 1)
                dve.tensor_scalar(thr[:, j:j + 1], pf[j][:, 0:1], 1.0 / (FF * C), 1e-8,
                                  ALU.mult, ALU.max).then_inc(s_wd, 1)
                dve.wait_ge(s_wd, n + 1)
                dve.tensor_scalar(half[:, j:j + 1], thr[:, j:j + 1], 0.5, None, ALU.mult)
                dve.tensor_scalar(nhalf[:, j:j + 1], thr[:, j:j + 1], -0.5, None, ALU.mult).then_inc(s_wd, 1)
                dve.wait_ge(s_wd, n + 2)
                dve.tensor_scalar(below, src[:, :], nhalf[:, j:j + 1], None, ALU.is_lt).then_inc(s_wd, 1)
                dve.wait_ge(s_wd, n + 3)
                dve.scalar_tensor_tensor(out=dst[:, :, :].rearrange("p k n -> p (k n)"), in0=src[:, :],
                                         scalar=half[:, j:j + 1], in1=below, op0=ALU.is_gt,
                                         op1=ALU.subtract).then_inc(s_wd, 1)

            def norm(g, n, src, dst):
                base = 6 * g + 3 * n
                for t in range(TG):
                    last = dve.bn_stats(stats[:, t, :], src[:, t, :])
                last.then_inc(s_ln, 1)
                dve.wait_ge(s_ln, base + 1)
                dve.memset(carrier[:, :], 0.0)
                for t in range(TG):
                    last = dve.bn_aggr(mv[:, t, :], stats[:, t, :])
                last.then_inc(s_ln, 1)
                dve.wait_ge(s_ln, base + 2)
                dve.wait_ge(s_rs, 4 * g + 2 * n + 2)
                for t in range(TG):
                    last = dve.tensor_scalar(dst[:, t, :], src[:, t, :], mv[:, t, 0:1], rstd[:, t:t + 1],
                                             ALU.subtract, ALU.mult)
                last.then_inc(s_ln, 1)
                dve.wait_ge(s_ln, base + 3)

            def norms(g):
                dve.wait_ge(s_x, 16 * (g + 1))
                wait(dve, s_tr, g)
                norm(g, 0, xin, xn)
                norm(g, 1, xn, zn)

            def operands(g):
                dve.wait_ge(s_tr, g + 1)
                wait(dve, s_x2, KC * g)
                for k in range(KC):
                    dve.wait_ge(s_x1, KC * g + k + 1)
                    dve.tensor_tensor(xr[:, k, :], tr_x[k], x1[:, k, :], ALU.subtract).then_inc(s_xr, 1)
                wait(dve, s_v, 2 * g)
                for k in range(KC):
                    dve.tensor_scalar(zt[:, k, :], tr_z[k], g_col[:, k:k + 1], b_col[:, k:k + 1],
                                      ALU.mult, ALU.add).then_inc(s_z, 1)
                for k in range(KC):
                    dve.wait_ge(s_x2, KC * g + k + 1)
                    dve.tensor_tensor(x3[:, k, :], xr[:, k, :], x2[:, k, :], ALU.subtract).then_inc(s_x3, 1)

            def q_rest(g):
                wait(dve, s_qs, 16 * KC * g)
                for k in range(KC):
                    dve.wait_ge(s_qa, 2 * (KC * g + k + 1))
                    dve.tensor_tensor(qr[:, k, :], qf[:, k, :], qp[:, k, 0, :], ALU.subtract).then_inc(s_qr, 1)

            def results(g, rows=None):

                def rest(i):
                    dve.wait_ge(s_g, 2 * (KF * g + 2 * i + 2))
                    dve.tensor_tensor(hid[:, 2 * i:2 * i + 2, :], hid[:, 2 * i:2 * i + 2, :],
                                      hp[0][:, 2 * i:2 * i + 2, :], ALU.subtract).then_inc(s_hr, 1)
                    if i % 2:
                        dve.wait_ge(s_hr, KF // 2 * g + i + 1)
                        dve.tensor_copy(hp[1][:, 2 * i:2 * i + 2, :], hid[:, 2 * i:2 * i + 2, :]).then_inc(s_h2[1], 1)

                def third(i):
                    dve.wait_ge(s_h2[i % 2], KF // 4 * g + i // 2 + 1)
                    dve.tensor_tensor(hp[2][:, 2 * i:2 * i + 2, :], hid[:, 2 * i:2 * i + 2, :],
                                      hp[1][:, 2 * i:2 * i + 2, :], ALU.subtract).then_inc(s_h3, 1)
                rest(0)
                for k in range(KC):
                    dve.wait_ge(s_q2, KC * g + k + 1)
                    dve.tensor_tensor(qp[:, k, 2, :], qr[:, k, :], qp[:, k, 1, :], ALU.subtract).then_inc(s_q3, 1)
                for i in range(1, KF // 2):
                    if rows:
                        rows(4)
                    rest(i)
                    third(i - 1)
                third(KF // 2 - 1)
                for t in range(TG):
                    dve.wait_ge(s_v, 2 * g + t // 2 + 1)
                    dve.tensor_tensor(v_all[:, ds(g * TG + t, 1), :].rearrange("p o c -> p (o c)"),
                                      pq[t // 2][:, (t % 2) * C:(t % 2 + 1) * C], bv_row[:, :], ALU.add).then_inc(s_vd, 1)

            def half_max(h, a):
                dve.wait_ge(s_a, NHALF * h + a + 1)
                dve.tensor_reduce(part_max[:, a // 2, a % 2:a % 2 + 1], pa[a % 2], AX.X, ALU.max).then_inc(s_r, 1)

            def split_max(h):
                dve.wait_ge(s_r, NHALF * (h + 1))
                dve.tensor_reduce(neg_max[:, :], part_max[:, :, :], AX.X, ALU.max, negate=True).then_inc(s_m, 1)
                wait(dve, s_mt, h)
                dve.wait_ge(s_m, 3 * h + 1)
                dve.tensor_copy(max_split[:, 0, :], neg_max[:, :]).then_inc(s_m, 1)
                dve.wait_ge(s_m, 3 * h + 2)
                dve.tensor_tensor(max_split[:, 1, :], neg_max[:, :], max_split[:, 0, :], ALU.subtract).then_inc(s_m, 1)

            dve.wait_ge(s_id, 16)
            dve.tensor_copy(idb[:, :], idf[:, :]).then_inc(s_idb, 1)
            norms(0)
            ternary(0, w1, w1t)
            dve.wait_ge(s_col, 64)
            operands(0)
            ternary(1, w2, w2t)
            q_rest(0)
            norms(1)
            dve.wait_ge(s_row, 49)
            results(0)
            with dve.Fori(1, NG - 1) as g:
                operands(g)
                norms(g + 1)
                q_rest(g)
                results(g)
            operands(NG - 1)
            q_rest(NG - 1)
            halves = iter(range(NHALF))

            def first_rows(n):
                for _ in range(n):
                    half_max(0, next(halves))
            results(NG - 1, first_rows)
            first_rows(NHALF - 4 * (KF // 2 - 1))
            split_max(0)

            with dve.Fori(1, NH) as h:
                for a in range(NHALF):
                    half_max(h, a)
                split_max(h)

            def recip(b):
                dve.wait_ge(s_sl, 16 * (b + 1))
                dve.reciprocal(rsum[b], sums[b]).then_inc(s_rc, 1)

            def add_resid(g, i, stored):
                wait(dve, s_out[i], 16 * stored)
                for t in range(0, TG, 2):
                    dve.wait_ge(s_y, 2 * g + t // 2 + 1)
                    dve.tensor_tensor(y[i][:, t:t + 2, :], py[t // 2].rearrange("p (t c) -> p t c", t=2),
                                      resid[:, ds(g * TG + t, 2), :], ALU.add).then_inc(s_yd, 1)

            def normalise(b, first):
                for c in range(NCH):
                    g = b * NCH + c
                    if first and c == 2:
                        recip(1)
                    dve.wait_ge(s_ol[c % 2], 32 * KC * (b * NCH // 2 + c // 2 + 1))
                    wait(dve, s_y, 2 * (g - 1))
                    for k in range(KC):
                        dve.tensor_tensor(on[c % 2][:, k, :], ot[c % 2][:, k, :], rb[c % 2][:, k, :],
                                          ALU.mult).then_inc(s_on, 1)
                    if c > 0 or not first:
                        add_resid(g - 1, (c - 1) % 2, b * (NCH // 2) + (c - 1) // 2)
            recip(0)
            normalise(0, True)
            with dve.Fori(1, NB) as b:
                normalise(b, False)
            add_resid(NG - 1, (NG - 1) % 2, (NG - 1) // 2)

        @block.scalar
        def _(act):
            act.dma_start(idf[:, :], ident).then_inc(s_id, 16)
            act.dma_start(w1[:, :].rearrange("p (k n) -> p k n", k=KC), w1_t.rearrange("(k p) n -> p k n", p=P)).then_inc(s_w[0], 16)
            for dst, src in ((g_col, ln_g), (b_col, ln_b), (bq_col, bq), (b1_col, b1)):
                act.dma_start(dst[:, :], src).then_inc(s_col, 16)
            for dst, src in ((bv_row, bv), (bo_row, bo), (b2_row, b2)):
                act.dma_start(dst[:, :], src.to_broadcast((P, C))).then_inc(s_row, 16)

            def abs_sum(j, w):
                act.wait_ge(s_w[j], 16)
                act.activation(hid[:, KF // 2 * j:KF // 2 * (j + 1), :].rearrange("p f n -> p (f n)"), w[:, :], ACT.Abs,
                               accum_out=wabs[:, j:j + 1]).then_inc(s_wa, 1)

            abs_sum(0, w1)
            abs_sum(1, w2)
            act.wait_ge(s_col, 64)

            def group(g, first):
                act.wait_ge(s_tr, g + 1)
                wait(act, s_h, KF * g)
                for k in range(KC):
                    act.activation(x1[:, k, :], tr_x[k], ACT.Copy).then_inc(s_x1, 1)
                for k in range(KC):
                    act.wait_ge(s_xr, KC * g + k + 1)
                    act.activation(x2[:, k, :], xr[:, k, :], ACT.Copy).then_inc(s_x2, 1)
                if not first:
                    ffn_out(g - 1)
                    act.wait_ge(s_q3, KC * g)
                    act.wait_ge(s_qs, 16 * KC * g)
                for k in range(KC):
                    act.wait_ge(s_q, KC * g + k + 1)
                    act.activation(qf[:, k, :], pq[k], ACT.Identity, bias=bq_col[:, k:k + 1]).then_inc(s_qa, 1)
                    act.activation(qp[:, k, 0, :], pq[k], ACT.Identity, bias=bq_col[:, k:k + 1]).then_inc(s_qa, 1)
                wait(act, s_h3, KF // 2 * g)
                for f in range(KF):
                    act.wait_ge(s_h, KF * g + f + 1)
                    act.activation(hid[:, f, :], pf[f % 2], ACT.Gelu, bias=b1_col[:, f:f + 1]).then_inc(s_g, 1)
                    if first and f == 0:
                        act.wait_ge(s_wd, 4)
                    act.activation(hp[0][:, f, :], pf[f % 2], ACT.Gelu, bias=b1_col[:, f:f + 1]).then_inc(s_g, 1)
                    if f == 1:
                        for k in range(KC):
                            act.wait_ge(s_qr, KC * g + k + 1)
                            act.activation(qp[:, k, 1, :], qr[:, k, :], ACT.Copy).then_inc(s_q2, 1)
                    if f % 4 == 3:
                        second(g, f // 2 - 1)

            def second(g, i):
                act.wait_ge(s_hr, KF // 2 * g + i + 1)
                if isinstance(g, int) and g == 0 and i == 0:
                    act.wait_ge(s_wd, 8)
                act.activation(hp[1][:, 2 * i:2 * i + 2, :], hid[:, 2 * i:2 * i + 2, :], ACT.Copy).then_inc(s_h2[0], 1)

            def ffn_out(g):
                for j in range(2):
                    act.wait_ge(s_f, 2 * g + j + 1)
                    if j == 0:
                        wait(act, s_ra, g)
                    act.activation(f2[:, 2 * j:2 * j + 2, :].rearrange("p t c -> p (t c)"), pf[j],
                                   ACT.Copy).then_inc(s_fe, 1)

            group(0, True)
            with act.Fori(1, NG) as g:
                group(g, False)
            ffn_out(NG - 1)

            def evacuate(h):
                act.wait_ge(s_pv, NBLK * (h + 1))
                wait(act, s_os, 16 * h)
                act.activation(o_sb, pv, ACT.Copy).then_inc(s_o, 1)

            def copy_max(h):
                act.wait_ge(s_mt, h + 1)
                wait(act, s_mr, 16 * h)
                act.activation(max_rows[:, :], pm[0:2 * NBLK, 0:P], ACT.Copy).then_inc(s_mc, 1)

            def head(h, first=False, last=False):
                for kb in range(NBLK):
                    for c in range(NCH):
                        act.wait_ge(s_b, NE * h + NCH * kb + c + 1)
                        if c == 0 and not (first and kb < 2):
                            act.wait_ge(s_pv, NBLK * h + kb - 1)
                        act.activation(prob[kb % 2][:, c * BANK:(c + 1) * BANK], ring_bank(NCH * kb + c, last), ACT.Exp,
                                       scale=SCALE).then_inc(s_e, 1)
                        if kb == 0 and c == 1 and not first:
                            evacuate(h - 1)
                    if kb == NBLK - AHEAD and not last:
                        copy_max(h + 1)
            copy_max(0)
            head(0, first=True)
            with act.Fori(1, NH - 1) as h:
                head(h)
            head(NH - 1, last=True)
            evacuate(NH - 1)

            with act.Fori(0, NB) as b:
                for c in range(NCH):
                    g = b * NCH + c
                    act.wait_ge(s_yd, 2 * (g + 1))
                    act.dma_start(out_v[ds(g, 1)].rearrange("o p t c -> (o p) t c"), y[c % 2]).then_inc(s_out[c % 2], 16)

        @block.tensor
        def _(pe):
            def ffn_down(g, t, between=None):
                for f in range(KF):
                    for i in range(3):
                        mm = pe.matmul(pf[t // 2][:, (t % 2) * C:(t % 2 + 1) * C], hp[i][:, f, t * P:(t + 1) * P],
                                       w2t[:, f, :], start=(f == 0 and i == 0), stop=(f == KF - 1 and i == 2))
                    if f == KF - 1 and t % 2:
                        mm.then_inc(s_f, 1)
                    if between and f % 2:
                        between()

            def abs_total(j):
                pe.wait_ge(s_wa, j + 1)
                pe.matmul(pf[j][:, 0:1], ones[:, :], wabs[:, j:j + 1], start=True, stop=True).then_inc(s_wp, 1)

            def group(g, between=None):
                pe.wait_ge(s_ln, 6 * g + 6)
                wait(pe, s_z, KC * g)
                wait(pe, s_xr, KC * g)
                for src, dst in ((xn, tr_x), (zn, tr_z)):
                    for k in range(KC):
                        for t in range(TG):
                            mm = pe.transpose(dst[k][:, t * P:(t + 1) * P], src[:, t, k * P:(k + 1) * P], idf[:, :])
                mm.then_inc(s_tr, 1)
                first = isinstance(g, int) and g == 0
                if not first:
                    pe.wait_ge(s_h3, KF // 2 * g)
                    for t in range(TG):
                        ffn_down(g - 1, t)
                wait(pe, s_vd, TG * g)
                for o in range(KC):
                    for k in range(KC):
                        if o == 0:
                            pe.wait_ge(s_z, KC * g + k + 1)
                        mm = pe.matmul(pq[o], wq[:, k, o * P:(o + 1) * P], zt[:, k, :], start=(k == 0), stop=(k == KC - 1))
                    mm.then_inc(s_q, 1)
                if first:
                    abs_total(1)
                    pe.wait_ge(s_wd, 5)

                def hidden(f, between=None):
                    if f < 2:
                        wait(pe, s_fe, 2 * (g - 1) + f + 1)
                    else:
                        pe.wait_ge(s_g, 2 * (KF * g + f - 1))
                    for k in range(KC):
                        for i, part in enumerate((x1, x2, x3)):
                            mm = pe.matmul(pf[f % 2], w1t[:, k, f * P:(f + 1) * P], part[:, k, :],
                                           start=(k == 0 and i == 0), stop=(k == KC - 1 and i == 2))
                        if k == KC - 1:
                            mm.then_inc(s_h, 1)
                        if between:
                            between()
                pe.wait_ge(s_x3, KC * (g + 1))
                hidden(0)
                hidden(1)
                for f in range(2, KF):
                    hidden(f, between)
                if first:
                    pe.wait_ge(s_wv, 16)
                pe.wait_ge(s_qa, 2 * KC * (g + 1))
                for t in range(TG):
                    for k in range(KC):
                        mm = pe.matmul(pq[t // 2][:, (t % 2) * C:(t % 2 + 1) * C], zt[:, k, t * P:(t + 1) * P],
                                       wv[:, k, :], start=(k == 0), stop=(k == KC - 1))
                    if t % 2:
                        mm.then_inc(s_v, 1)

            pe.wait_ge(s_id, 16)
            pe.wait_ge(s_c, 1)
            abs_total(0)
            pe.wait_ge(s_wq, 16)
            group(0)
            with pe.Fori(1, NG - 1) as g:
                group(g)

            pe.wait_ge(s_pc, 3 + ROT)

            halves = iter([(0, a) for a in range(NHALF)] + [(1, a) for a in range(2 * AHEAD)])

            def first_a():
                h, a = next(halves, (None, None))
                if h is None:
                    return
                if (h, a) == (0, 0):
                    pe.wait_ge(s_z, KC * NG)
                    pe.wait_ge(s_xr, KC * NG)
                if a == 0:
                    pe.wait_ge(s_ld[h], 96)
                a_half(pe, h, h, a)

            group(NG - 1, first_a)
            pe.wait_ge(s_h3, KF // 2 * NG)
            for t in range(TG):
                ffn_down(NG - 1, t, first_a)
            for _ in range(NHALF):
                first_a()
            pe.wait_ge(s_idb, 1)
            pe.wait_ge(s_vd, TG * NG)
            pe.wait_ge(s_fe, 2 * NG)
            max_transpose(pe, 0)
            pe_head(pe, 0, 0)
            n_it = (NH - 3) // ROT
            with pe.Fori(0, n_it) as j:
                for k in range(1, ROT + 1):
                    pe_head(pe, j, k)
            for h in range(1 + n_it * ROT, NH):
                pe_head(pe, 0, h)

            pe.wait_ge(s_wo, 16)
            def project(b):
                for c in range(NCH):
                    g = b * NCH + c
                    pe.wait_ge(s_on, KC * (g + 1))
                    for t in range(TG):
                        if t % 2 == 0:
                            wait(pe, s_yd, 2 * g + t // 2 - 1)
                        for k in range(KC):
                            mm = pe.matmul(py[t // 2][:, (t % 2) * C:(t % 2 + 1) * C], on[c % 2][:, k, t * P:(t + 1) * P],
                                           wo[:, k, :], start=(k == 0), stop=(k == KC - 1))
                        if t % 2:
                            mm.then_inc(s_y, 1)
            project(0)
            with pe.Fori(1, NB) as b:
                project(b)


def kernel(L0_attn_x, L0_attn_ln1_g, L0_attn_ln1_b, L0_attn_w_in, L0_attn_b_in, L0_attn_w_out, L0_attn_b_out,
           L0_ffn_W1, L0_ffn_b1, L0_ffn_W2, L0_ffn_b2):
    import numpy as np
    import concourse.bacc as bacc
    from concourse.bass_utils import run_bass_kernel_spmd

    c = L0_attn_x.shape[2]

    def array(a):
        return np.ascontiguousarray(np.asarray(a))

    def columns(v):
        return array(np.asarray(v).reshape(-1, P).T)

    w_in, b_in = np.asarray(L0_attn_w_in), np.asarray(L0_attn_b_in)
    arrays = {
        "x": array(L0_attn_x),
        "ln_g": columns(L0_attn_ln1_g), "ln_b": columns(L0_attn_ln1_b),
        "wq_t": array(w_in[0:c].T), "wv_t": array(w_in[2 * c:3 * c].T), "wo_t": array(np.asarray(L0_attn_w_out).T),
        "bq": columns(b_in[0:c]), "bv": array(b_in[None, 2 * c:3 * c]), "bo": array(np.asarray(L0_attn_b_out)[None, :]),
        "w1_t": array(np.asarray(L0_ffn_W1).T), "b1": columns(L0_ffn_b1),
        "w2_t": array(np.asarray(L0_ffn_W2).T), "b2": array(np.asarray(L0_ffn_b2)[None, :]),
        "ident": np.eye(P, dtype=np.float32),
    }
    nc = bacc.Bacc("TRN2", target_bir_lowering=False, num_devices=1)
    args = [nc.dram_tensor(f"in_{n}", a.shape, mybir.dt.from_np(a.dtype), kind="ExternalInput").ap()
            for n, a in arrays.items()]
    out = nc.dram_tensor("out", tuple(L0_attn_x.shape), F32, kind="ExternalOutput").ap()
    attention_ffn(nc, *args, out)
    r = run_bass_kernel_spmd(nc, [{f"in_{n}": a for n, a in arrays.items()}], core_ids=[0])
    return r.results[0]["out"]
```

```python
from contextlib import ExitStack

import concourse.bass as bass
from concourse import mybir

F32 = mybir.dt.float32
BF16 = mybir.dt.bfloat16
ALU = mybir.AluOpType
ACT = mybir.ActivationFunctionType
AX = mybir.AxisListType
ds = bass.ds

P = 128
EPS = 1e-5
BANK = 512

KEY_PARTS = (0, 1, 2, 0, 1, 0)
QRY_PARTS = (0, 0, 0, 1, 1, 2)
ROT = 3

AHEAD = 2
PERIOD = "BABBPBABBBABP"
PERIOD_MAX = "BBBPAABBABAPBAB"
PERIOD_NEXT = "BBABPBBBAPBAB"
PERIOD_LAST = "BBBBPBBBBP"


def wait(eng, sem, value):
    if not isinstance(value, int) or value > 0:
        eng.wait_ge(sem, value)


def attention_ffn(nc, x, ln_g, ln_b, wq_t, wv_t, wo_t, bq, bv, bo, w1_t, b1, w2_t, b2, ident, out):
    NB, L, C = x.shape
    FF = w1_t.shape[1]
    D = 16
    H = C // D
    NH = NB * H
    KC = C // P
    KF = FF // P
    NBLK = L // P
    NCH = L // BANK
    TG = BANK // P
    NT = NB * L // P
    NG = NT // TG
    HC = P // D
    NPER = NBLK // 2
    NHALF = 3 * NPER
    NA = NHALF + 2
    NE = NBLK * NCH
    SPLIT = len(KEY_PARTS) * D
    KROWS = SPLIT + 2
    W = 2 * BANK
    SCALE = 1.0 / float(D) ** 0.5
    assert NCH == 4 and NB == 2 and NH > 2 * ROT

    x_v = x.rearrange("b (g t p) c -> (b g) p t c", t=TG, p=P)
    out_v = out.rearrange("b (g t p) c -> (b g) p t c", t=TG, p=P)
    q_dram = nc.dram_tensor("q_parts", (3, C, NB * L), BF16, kind="Internal").ap()
    o_dram = nc.dram_tensor("o_heads", (NH, NCH, 2 * D, BANK), F32, kind="Internal").ap()
    r_dram = nc.dram_tensor("o_recip", (NH, NCH, BANK), F32, kind="Internal").ap()

    ctx = ExitStack()
    with ctx:
        def sb(name, shape, dt=F32):
            return ctx.enter_context(nc.sbuf_tensor(name, shape, dt))

        def sem(name):
            return ctx.enter_context(nc.semaphore(name))

        wq = sb("wq", [P, KC, C])
        wv = sb("wv", [P, KC, C])
        wo = sb("wo", [P, KC, C])
        w1 = sb("w1", [P, KC * FF])
        w2 = sb("w2", [P, KF * C])
        w1t = sb("w1_ternary", [P, KC, FF], BF16)
        w2t = sb("w2_ternary", [P, KF, C], BF16)
        idf = sb("ident_f32", [P, P])
        idb = sb("ident_bf16", [P, P], BF16)
        ones = sb("ones", [P, P])
        g_col = sb("g_col", [P, KC])
        b_col = sb("b_col", [P, KC])
        bq_col = sb("bq_col", [P, KC])
        b1_col = sb("b1_col", [P, KF])
        bv_row = sb("bv_row", [P, C])
        bo_row = sb("bo_row", [P, C])
        b2_row = sb("b2_row", [P, C])
        bias_row = sb("bias_row", [P, C])
        wabs = sb("wabs", [P, 2])
        thr = sb("thr", [P, 2])
        half = sb("half", [P, 2])
        nhalf = sb("nhalf", [P, 2])
        expo = sb("minus_half", [P, TG])
        xin = sb("xin", [P, TG, C])
        xn = sb("xn", [P, TG, C])
        zn = sb("zn", [P, TG, C])
        stats = sb("stats", [P, TG, 6])
        mv = sb("mean_var", [P, TG, 2])
        carrier = sb("wait_carrier", [P, 1])
        eps = sb("eps", [P, TG])
        veps = sb("var_eps", [P, TG])
        rstd = sb("rstd", [P, TG])
        x1 = sb("x1", [P, KC, BANK], BF16)
        x2 = sb("x2", [P, KC, BANK], BF16)
        x3 = sb("x3", [P, KC, BANK], BF16)
        xr = sb("x_rest", [P, KC, BANK])
        zt = sb("zt", [P, KC, BANK])
        qf = sb("qf", [P, KC, BANK])
        qr = sb("q_rest", [P, KC, BANK])
        qp = sb("q_split", [P, KC, 3, BANK], BF16)
        hid = sb("hidden", [P, KF, BANK])
        hid3 = sb("hidden3", [P, KF, BANK], BF16)
        hp = [w1[:, :].bitcast(BF16).rearrange("p (f n) -> p f n", f=KF),
              w2[:, :].bitcast(BF16).rearrange("p (f n) -> p f n", f=KF), hid3]
        below = hid3[:, :, :].rearrange("p f n -> p (f n)").bitcast(F32)
        f2 = sb("ffn_out", [P, TG, C])
        resid = sb("resid", [P, NT, C])
        v_all = sb("v_all", [P, NT, C])
        key = [sb(f"key{i}", [P, L], BF16) for i in range(ROT)]
        qry = [sb(f"qry{i}", [P, L], BF16) for i in range(ROT)]
        vst = sb("v_ones", [P, NBLK, 2 * D])
        prob = [w1, w2]
        run_max = sb("run_max", [P, W])
        part_max = sb("part_max", [P, NBLK, 2])
        neg_max = sb("neg_max", [P, NBLK])
        max_split = sb("max_split", [P, 2, NBLK], BF16)
        max_rows = sb("max_rows", [2 * NBLK, P], BF16)
        o_sb = xin[:, 0:2, :].rearrange("p t c -> p (t c)")
        pieces = [(0, H), (H, NH - 1), (NH - 1, NH)]
        piece_shape = [(P, L // P) if h1 - h0 == 1 else (P // H * (h1 - h0), L * H // P) for h0, h1 in pieces]
        sums, rsum = ([z[0:rows, n, 0:cols] for n, (rows, cols) in enumerate(piece_shape)] for z in (xn, zn))
        ot = [hid[:, KC * i:KC * (i + 1), :] for i in range(2)]
        rb = [hid[:, KC * (i + 2):KC * (i + 3), :] for i in range(2)]
        on = [xr, qf]
        y = [z[:, :, :].rearrange("p k (t c) -> p (k t) c", c=C) for z in (zt, qr)]

        ps = ctx.enter_context(nc.psum_tensor("ps", [P, 8 * BANK], F32))

        def bank(b, n=1):
            return ps[:, b * BANK:(b + n) * BANK]
        tr_x = [bank(0), bank(1)]
        tr_z = [bank(2), bank(3)]
        pq = [bank(4), bank(5)]
        pf = [bank(6), bank(7)]
        pa = [bank(0, 2), bank(2, 2)]
        pb = [bank(4), bank(5), bank(7)]
        pb_last = pb + [bank(0), bank(1)]
        pm = pb[0][:, 0:P // 2].bitcast(BF16)
        pv = bank(6)
        py = [bank(2), bank(3)]

        s_id = sem("ident_loaded")
        s_col = sem("columns_loaded")
        s_row = sem("rows_loaded")
        s_wq = sem("wq_loaded")
        s_wv = sem("wv_loaded")
        s_wo = sem("wo_loaded")
        s_w = [sem("w1_loaded"), sem("w2_loaded")]
        s_c = sem("ones_done")
        s_pc = sem("pool_constants")
        s_x = sem("x_loaded")
        s_idb = sem("ident_bf16_done")
        s_wa = sem("weight_abs_sums")
        s_wp = sem("weight_scales")
        s_wd = sem("weight_dve")
        s_ln = sem("ln_dve")
        s_rs = sem("ln_pool")
        s_xb = sem("x_plus_bias")
        s_tr = sem("transposed")
        s_x1 = sem("x1")
        s_xr = sem("x_rest_done")
        s_x2 = sem("x2")
        s_x3 = sem("x3")
        s_z = sem("zt_done")
        s_q = sem("q_psum")
        s_qa = sem("q_biased")
        s_qr = sem("q_rest_done")
        s_q2 = sem("q2")
        s_q3 = sem("q3")
        s_qs = sem("q_stored")
        s_v = sem("v_psum")
        s_vd = sem("v_done")
        s_h = sem("hidden_psum")
        s_g = sem("gelu_done")
        s_hr = sem("hidden_rest")
        s_h2 = [sem("hidden2_even"), sem("hidden2_odd")]
        s_h3 = sem("hidden3_done")
        s_f = sem("ffn_psum")
        s_fe = sem("ffn_evacuated")
        s_ra = sem("resid_done")
        s_ld = [sem(f"head_loaded{i}") for i in range(ROT)]
        s_a = sem("pass_a")
        s_r = sem("row_max")
        s_m = sem("max_dve")
        s_mt = sem("max_transposed")
        s_mc = sem("max_copied")
        s_mr = sem("max_rows_in_place")
        s_b = sem("pass_b")
        s_e = sem("exp_done")
        s_vs = sem("v_staged")
        s_pv = sem("pv_done")
        s_o = sem("o_evacuated")
        s_os = sem("o_stored")
        s_sl = sem("sums_loaded")
        s_rc = sem("recip_done")
        s_rw = sem("recip_stored")
        s_ol = [sem(f"o_loaded{i}") for i in range(2)]
        s_on = sem("o_normalised")
        s_y = sem("y_psum")
        s_yd = sem("y_done")
        s_out = [sem(f"out_stored{i}") for i in range(2)]

        EARLY = 6

        def a_block(a):
            i, r = a // 3, a % 3
            return (i + NPER if r == 1 else i), (0 if r == 0 else 1)

        def a_step(eng, h, v, a):
            pair = pa[a % 2]
            if a < NHALF:
                wait(eng, s_r, NA * h + a - 1)
                blk, half_ = a_block(a)
                for j in range(2):
                    col = half_ * W + j * BANK
                    mm = eng.matmul(pair[:, j * BANK:(j + 1) * BANK], key[v][0:SPLIT, blk * P:(blk + 1) * P],
                                    qry[v][0:SPLIT, col:col + BANK], start=True, stop=True)
            else:
                eng.wait_ge(s_r, NA * h + NHALF)
                for t in range(NCH):
                    col = (a - NHALF) * BANK + t * P
                    mm = eng.transpose(pair[:, t * P:(t + 1) * P], run_max[:, col:col + P], idf[:, :])
            mm.then_inc(s_a, 1)

        MAX_AT = 54
        EVAC_AT = 2
        assert (NE + 2) % len(pb) == 0 and MAX_AT % len(pb) == 0

        def turn(i):
            return i if i < MAX_AT else i + 2

        def ring_bank(i, last):
            return pb_last[i % len(pb_last)] if last else pb[turn(i) % len(pb)]

        def max_transpose(eng, h):
            eng.wait_ge(s_m, 3 * h + 3)
            wait(eng, s_e, NE * (h - 1) + MAX_AT - len(pb) + 1)
            eng.transpose(pm[0:2 * NBLK, 0:P], max_split[:, :, :].rearrange("p s k -> p (s k)"), idb[:, :]).then_inc(s_mt, 1)

        def pv_block(eng, h, kb):
            eng.wait_ge(s_e, NE * h + NCH * (kb + 1))
            if kb % (NBLK // 2) == 0:
                eng.wait_ge(s_vs, 2 * h + 1 + kb // (NBLK // 2))
            if kb == 0:
                wait(eng, s_o, h)
            for c in range(NCH):
                mm = eng.matmul(pv[32 * c:32 * c + 2 * D, :], vst[:, kb, :],
                                prob[kb % 2][:, c * BANK:(c + 1) * BANK],
                                start=(kb == 0), stop=(kb == NBLK - 1))
            mm.then_inc(s_pv, 1)

        def b_chunk(eng, h, v, kb, c, last):
            i = NCH * kb + c
            if i == 0:
                eng.wait_ge(s_mr, 16 * (h + 1))
            before = turn(i) - len(pb)
            if last and i >= len(pb):
                if i >= len(pb_last):
                    eng.wait_ge(s_e, NE * h + i - len(pb_last) + 1)
            elif before == MAX_AT:
                eng.wait_ge(s_mc, h + 2)
            elif before < MAX_AT:
                wait(eng, s_e, NE * h + before + 1)
            elif before == MAX_AT + 1:
                eng.wait_ge(s_e, NE * h + before - len(pb) + 1)
            else:
                eng.wait_ge(s_e, NE * h + before - 1)
            eng.matmul(ring_bank(i, last), key[v][0:KROWS, kb * P:(kb + 1) * P],
                       qry[v][0:KROWS, c * BANK:(c + 1) * BANK], start=True, stop=True).then_inc(s_b, 1)

        def pe_head(eng, j, k):
            h = j * ROT + k
            static = isinstance(h, int)
            first = static and h == 0
            left = NH - 1 - h if static else ROT
            last = left == 0
            if last:
                eng.wait_ge(s_r, NA * NH)
            i, kb = 0, -1
            for q in range(NPER):
                steps = iter([(1 if q + AHEAD < NPER else 2, 3 * ((q + AHEAD) % NPER) + n) for n in range(3)])
                pattern = PERIOD
                if q + AHEAD == NPER:
                    pattern = PERIOD_MAX
                    steps = iter([(1, NHALF), (1, NHALF + 1)] + list(steps))
                elif q + AHEAD == NPER + 1:
                    pattern = PERIOD_NEXT
                if last:
                    pattern = PERIOD_LAST
                for what in pattern:
                    if what == "B":
                        if i == MAX_AT and not last:
                            max_transpose(eng, h + 1)
                        b_chunk(eng, h, k % ROT, i // NCH, i % NCH, last)
                        i += 1
                    elif what == "P":
                        if kb >= 0:
                            pv_block(eng, h, kb)
                        elif not first:
                            pv_block(eng, h - 1, NBLK - 1)
                        kb += 1
                    else:
                        ahead, a = next(steps)
                        if left >= ahead:
                            if a == 0:
                                eng.wait_ge(s_ld[(k + ahead) % ROT], 96 * (j + (k + ahead) // ROT + 1))
                            a_step(eng, h + ahead, (k + ahead) % ROT, a)
            if last:
                pv_block(eng, h, NBLK - 1)

        def project(eng, g, t):
            if t == 0:
                eng.wait_ge(s_on, KC * (g + 1))
            if t % 2 == 0:
                wait(eng, s_yd, 2 * g + t // 2 - 1)
            for k in range(KC):
                mm = eng.matmul(py[t // 2][:, (t % 2) * C:(t % 2 + 1) * C], on[g % 2][:, k, t * P:(t + 1) * P],
                                      wo[:, k, :], start=(k == 0), stop=(k == KC - 1))
            if t % 2:
                mm.then_inc(s_y, 1)

        block = ctx.enter_context(nc.Block())

        @block.sync
        def _(sp):
            sp.dma_start(xin[:, :, :], x_v[0]).then_inc(s_x, 16)
            for dst, src, s in ((wq[:, :, :], wq_t, s_wq), (w2[:, :].rearrange("p (k n) -> p k n", k=KF), w2_t, s_w[1]),
                                (wv[:, :, :], wv_t, s_wv), (wo[:, :, :], wo_t, s_wo)):
                sp.dma_start(dst, src.rearrange("(k p) n -> p k n", p=P)).then_inc(s, 16)

            def store_q(g):
                sp.wait_ge(s_q3, g + 1)
                for k in range(KC):
                    sp.dma_start(q_dram[:, k * P:(k + 1) * P, ds(g * BANK, BANK)].rearrange("s p n -> p s n"),
                                 qp[:, k, :, :]).then_inc(s_qs, 16)

            with sp.Fori(1, NG) as g:
                sp.wait_ge(s_ln, 6 * g)
                sp.wait_ge(s_xb, g)
                sp.dma_start(xin[:, :, :], x_v[ds(g, 1)].rearrange("o p t c -> (o p) t c")).then_inc(s_x, 16)
                store_q(g - 1)

            def load_head(h, v):
                b, hh = h // H, h % H
                src = q_dram[:, ds(hh * D, D), ds(b * L, L)]
                sp.dma_start(key[v][0:3 * D, :], src).then_inc(s_ld[v], 16)
                sp.dma_start(key[v][3 * D:5 * D, :], src[0:2]).then_inc(s_ld[v], 16)
                sp.dma_start(key[v][5 * D:6 * D, :], src[0]).then_inc(s_ld[v], 16)
                at = 0
                for part, times in ((0, 3), (1, 2), (2, 1)):
                    one = src[part:part + 1].to_broadcast((times, D, L)) if times > 1 else src[part]
                    sp.dma_start(qry[v][at * D:(at + times) * D, :], one).then_inc(s_ld[v], 16)
                    at += times

            def max_rows_in(h, v):
                sp.wait_ge(s_mc, h + 1)
                sp.dma_start(qry[v][SPLIT:KROWS, :].rearrange("s (k p) -> s k p", p=P), max_rows[:, :]).then_inc(s_mr, 16)

            def store_o(h):
                sp.wait_ge(s_o, h + 1)
                sp.dma_start(o_dram[ds(h, 1)].rearrange("h c r n -> (h c r) n"), o_sb).then_inc(s_os, 16)

            load_head(0, 0)
            load_head(1, 1)
            store_q(NG - 1)
            sp.wait_ge(s_qs, 16 * KC * NG)
            max_rows_in(0, 0)
            load_head(2, 2)
            max_rows_in(1, 1)

            def sp_head(h, i):
                sp.wait_ge(s_b, NE * h)
                load_head(h + 2, (i + 2) % ROT)
                store_o(h - 1)
                max_rows_in(h + 1, (i + 1) % ROT)
            n_it = (NH - 3) // ROT
            with sp.Fori(0, n_it) as j:
                for u in range(ROT):
                    sp_head(j * ROT + (u + 1), u + 1)
            for h in range(1 + n_it * ROT, NH):
                if h + 2 < NH:
                    sp_head(h, h)
                elif h + 1 < NH:
                    store_o(h - 1)
                    max_rows_in(h + 1, (h + 1) % ROT)

            def spread_recip(n):
                h0, h1 = pieces[n]
                if h1 == NH:
                    for c in range(NCH):
                        sp.dma_start(sums[n][c * P // NCH:(c + 1) * P // NCH, :],
                                     o_sb[2 * D * c + D:2 * D * c + D + 1, :]).then_inc(s_sl, 16)
                else:
                    sp.wait_ge(s_os, 16 * h1)
                    sp.dma_start(sums[n], o_dram[h0:h1, :, D, :].rearrange("h c n -> (h c) n")).then_inc(s_sl, 16)
                sp.wait_ge(s_rc, n + 1)
                sp.dma_start(r_dram[h0:h1].rearrange("h c n -> (h c) n"), rsum[n]).then_inc(s_rw, 16)
                sp.wait_ge(s_rw, 16 * (n + 1))

            def load_o(g):
                b, c = g // NCH, g % NCH
                for k in range(KC):
                    wait(sp, s_on, KC * (g - 2) + k + 1)
                    h0 = b * H + k * HC
                    sp.dma_start(ot[c % 2][:, k, :], o_dram[h0:h0 + HC, c, 0:D, :]).then_inc(s_ol[c % 2], 16)
                    sp.dma_start(rb[c % 2][:, k, :],
                                 r_dram[h0:h0 + HC, c:c + 1, :].to_broadcast((HC, D, BANK))).then_inc(s_ol[c % 2], 16)

            spread_recip(0)
            load_o(0)
            load_o(1)
            store_o(NH - 2)
            spread_recip(1)
            load_o(2)
            load_o(3)
            store_o(NH - 1)
            spread_recip(2)
            for g in range(NCH, NG):
                load_o(g)
            for i in range(2):
                sp.wait_ge(s_out[i], 16 * NG // 2)

        @block.gpsimd
        def _(pool):
            sets = [(expo[:, :], -0.5), (eps[:, :], EPS), (vst[:, :, :], 1.0)] + [(k[SPLIT:P, :], 1.0) for k in key]

            def constants(n0, n1):
                for n in range(n0, n1):
                    dst, value = sets[n]
                    pool.memset(dst, value).then_inc(s_pc, 1)
                    pool.wait_ge(s_pc, n + 1)

            def rsqrt(g):
                for n in range(2):
                    pool.wait_ge(s_ln, 6 * g + 3 * n + 2)
                    pool.tensor_tensor(veps[:, :], mv[:, :, 1], eps[:, :], ALU.add).then_inc(s_rs, 1)
                    pool.wait_ge(s_rs, 4 * g + 2 * n + 1)
                    pool.tensor_tensor(rstd[:, :], veps[:, :], expo[:, :], ALU.pow).then_inc(s_rs, 1)

            def group(g, add=True):
                rsqrt(g)
                residual(g, add)

            def residual(g, add=True):
                for t in range(TG):
                    last = pool.tensor_tensor(resid[:, ds(g * TG + t, 1), :].rearrange("p o c -> p (o c)"),
                                              xin[:, t, :], bias_row[:, :], ALU.add)
                last.then_inc(s_xb, 1)
                if add:
                    add_ffn(g - 2)

            def add_ffn(g):
                pool.wait_ge(s_fe, 2 * (g + 1))
                pool.wait_ge(s_xb, g + 1)
                pool.tensor_tensor(resid[:, ds(g * TG, TG), :], resid[:, ds(g * TG, TG), :], f2[:, :, :],
                                   ALU.add).then_inc(s_ra, 1)

            constants(0, 2)
            rsqrt(0)
            pool.wait_ge(s_row, 48)
            pool.tensor_tensor(bias_row[:, :], bo_row[:, :], b2_row[:, :], ALU.add).then_inc(s_row, 1)
            pool.wait_ge(s_row, 49)
            residual(0, add=False)
            group(1, add=False)
            constants(2, len(sets))
            with pool.Fori(2, NG) as g:
                group(g)

            def stage(h, n):
                b, hh = h // H, h % H
                k0 = n * NBLK // 2
                pool.tensor_copy(vst[:, k0:k0 + NBLK // 2, 0:D],
                                 v_all[:, ds(b * NBLK + k0, NBLK // 2), ds(hh * D, D)]).then_inc(s_vs, 1)
            pool.wait_ge(s_vd, TG * NG)
            stage(0, 0)
            stage(0, 1)
            add_ffn(NG - 2)
            add_ffn(NG - 1)
            with pool.Fori(1, NH) as h:
                for n in range(2):
                    pool.wait_ge(s_pv, NBLK * h - NBLK // 2 * (1 - n))
                    stage(h, n)

        @block.vector
        def _(dve):
            dve.memset(ones[:, :], 1.0).then_inc(s_c, 1)

            def ternary(j, src, dst):
                n = 4 * j
                dve.wait_ge(s_wp, j + 1)
                dve.tensor_scalar(thr[:, j:j + 1], pf[j][:, 0:1], 1.0 / (FF * C), 1e-8,
                                  ALU.mult, ALU.max).then_inc(s_wd, 1)
                dve.wait_ge(s_wd, n + 1)
                dve.tensor_scalar(half[:, j:j + 1], thr[:, j:j + 1], 0.5, None, ALU.mult)
                dve.tensor_scalar(nhalf[:, j:j + 1], thr[:, j:j + 1], -0.5, None, ALU.mult).then_inc(s_wd, 1)
                dve.wait_ge(s_wd, n + 2)
                dve.tensor_scalar(below, src[:, :], nhalf[:, j:j + 1], None, ALU.is_lt).then_inc(s_wd, 1)
                dve.wait_ge(s_wd, n + 3)
                dve.scalar_tensor_tensor(out=dst[:, :, :].rearrange("p k n -> p (k n)"), in0=src[:, :],
                                         scalar=half[:, j:j + 1], in1=below, op0=ALU.is_gt,
                                         op1=ALU.subtract).then_inc(s_wd, 1)

            def norm(g, n, src, dst):
                base = 6 * g + 3 * n
                for t in range(TG):
                    last = dve.bn_stats(stats[:, t, :], src[:, t, :])
                last.then_inc(s_ln, 1)
                dve.wait_ge(s_ln, base + 1)
                dve.memset(carrier[:, :], 0.0)
                for t in range(TG):
                    last = dve.bn_aggr(mv[:, t, :], stats[:, t, :])
                last.then_inc(s_ln, 1)
                dve.wait_ge(s_ln, base + 2)
                dve.wait_ge(s_rs, 4 * g + 2 * n + 2)
                for t in range(TG):
                    last = dve.tensor_scalar(dst[:, t, :], src[:, t, :], mv[:, t, 0:1], rstd[:, t:t + 1],
                                             ALU.subtract, ALU.mult)
                last.then_inc(s_ln, 1)
                dve.wait_ge(s_ln, base + 3)

            def norm_ready(g):
                dve.wait_ge(s_x, 16 * (g + 1))
                wait(dve, s_tr, g)

            def norms(g):
                norm_ready(g)
                norm(g, 0, xin, xn)
                norm(g, 1, xn, zn)

            def operands(g):
                dve.wait_ge(s_tr, g + 1)
                wait(dve, s_x2, KC * g)
                for k in range(KC):
                    dve.wait_ge(s_x1, KC * g + k + 1)
                    dve.tensor_tensor(xr[:, k, :], tr_x[k], x1[:, k, :], ALU.subtract).then_inc(s_xr, 1)
                wait(dve, s_v, 2 * g)
                for k in range(KC):
                    dve.tensor_scalar(zt[:, k, :], tr_z[k], g_col[:, k:k + 1], b_col[:, k:k + 1],
                                      ALU.mult, ALU.add).then_inc(s_z, 1)
                for k in range(KC):
                    dve.wait_ge(s_x2, KC * g + k + 1)
                    dve.tensor_tensor(x3[:, k, :], xr[:, k, :], x2[:, k, :], ALU.subtract).then_inc(s_x3, 1)

            def q_split(g):
                wait(dve, s_qs, 16 * KC * g)
                for k in range(KC):
                    dve.wait_ge(s_qa, 2 * (KC * g + k + 1))
                    dve.tensor_tensor(qr[:, k, :], qf[:, k, :], qp[:, k, 0, :], ALU.subtract).then_inc(s_qr, 1)
                dve.wait_ge(s_qr, KC * (g + 1))
                dve.tensor_copy(qp[:, :, 1, :], qr[:, :, :]).then_inc(s_q2, 1)
                dve.wait_ge(s_q2, g + 1)
                dve.tensor_tensor(qp[:, :, 2, :], qr[:, :, :], qp[:, :, 1, :], ALU.subtract).then_inc(s_q3, 1)

            def results(g, rows=None):
                def rest(i):
                    dve.wait_ge(s_g, 2 * (KF * g + 2 * i + 2))
                    dve.tensor_tensor(hid[:, 2 * i:2 * i + 2, :], hid[:, 2 * i:2 * i + 2, :],
                                      hp[0][:, 2 * i:2 * i + 2, :], ALU.subtract).then_inc(s_hr, 1)
                    if i % 2:
                        dve.wait_ge(s_hr, KF // 2 * g + i + 1)
                        dve.tensor_copy(hp[1][:, 2 * i:2 * i + 2, :], hid[:, 2 * i:2 * i + 2, :]).then_inc(s_h2[1], 1)

                def third(i):
                    dve.wait_ge(s_h2[i % 2], KF // 4 * g + i // 2 + 1)
                    dve.tensor_tensor(hp[2][:, 2 * i:2 * i + 2, :], hid[:, 2 * i:2 * i + 2, :],
                                      hp[1][:, 2 * i:2 * i + 2, :], ALU.subtract).then_inc(s_h3, 1)
                rest(0)
                for i in range(1, KF // 2):
                    if rows:
                        rows(2)
                    rest(i)
                    third(i - 1)
                third(KF // 2 - 1)
                for t in range(TG):
                    dve.wait_ge(s_v, 2 * g + t // 2 + 1)
                    dve.tensor_tensor(v_all[:, ds(g * TG + t, 1), :].rearrange("p o c -> p (o c)"),
                                      pq[t // 2][:, (t % 2) * C:(t % 2 + 1) * C], bv_row[:, :], ALU.add).then_inc(s_vd, 1)

            def max_step(h, a):
                dve.wait_ge(s_a, NA * h + a + 1)
                pair = pa[a % 2]
                if a < NHALF:
                    blk, half_ = a_block(a)
                    op = dve.tensor_reduce(part_max[:, blk, half_:half_ + 1], pair, AX.X, ALU.max)
                    if a == 2:
                        op = dve.tensor_copy(run_max[:, :], pair)
                    elif a % 3 == 2:
                        dve.wait_ge(s_r, NA * h + a - 2)
                        op = dve.tensor_tensor(run_max[:, :], run_max[:, :], pair, ALU.max)
                else:
                    t0 = NPER + (a - NHALF) * NCH
                    op = dve.tensor_reduce(part_max[:, t0:t0 + NCH, 0],
                                           pair[:, 0:BANK].rearrange("p (t n) -> p t n", n=P), AX.X, ALU.max)
                op.then_inc(s_r, 1)

            def split_max(h):
                dve.wait_ge(s_r, NA * (h + 1))
                dve.tensor_reduce(neg_max[:, :], part_max[:, :, :], AX.X, ALU.max, negate=True).then_inc(s_m, 1)
                wait(dve, s_mt, h)
                dve.wait_ge(s_m, 3 * h + 1)
                dve.tensor_copy(max_split[:, 0, :], neg_max[:, :]).then_inc(s_m, 1)
                dve.wait_ge(s_m, 3 * h + 2)
                dve.tensor_tensor(max_split[:, 1, :], neg_max[:, :], max_split[:, 0, :], ALU.subtract).then_inc(s_m, 1)

            dve.wait_ge(s_id, 16)
            dve.tensor_copy(idb[:, :], idf[:, :]).then_inc(s_idb, 1)
            norms(0)
            ternary(0, w1, w1t)
            dve.wait_ge(s_col, 64)
            operands(0)
            ternary(1, w2, w2t)
            norm_ready(1)
            norm(1, 0, xin, xn)
            q_split(0)
            norm(1, 1, xn, zn)
            dve.wait_ge(s_row, 49)
            results(0)
            with dve.Fori(1, NG - 1) as g:
                operands(g)
                norms(g + 1)
                q_split(g)
                results(g)
            operands(NG - 1)
            steps = iter(range(NA))

            def first_rows(n):
                for _ in range(n):
                    max_step(0, next(steps))
            first_rows(EARLY)
            q_split(NG - 1)
            results(NG - 1, first_rows)
            first_rows(NA - EARLY - 2 * (KF // 2 - 1))
            split_max(0)

            with dve.Fori(1, NH) as h:
                for a in range(NA):
                    max_step(h, a)
                split_max(h)

            def recip(n):
                last_piece = n == len(pieces) - 1
                dve.wait_ge(s_sl, 16 * (n + (NCH if last_piece else 1)))
                dve.reciprocal(rsum[n], sums[n]).then_inc(s_rc, 1)

            def add_resid(g):
                i = g % 2
                wait(dve, s_out[i], 16 * (g // 2))
                for t in range(0, TG, 2):
                    dve.wait_ge(s_y, 2 * g + t // 2 + 1)
                    dve.tensor_tensor(y[i][:, t:t + 2, :], py[t // 2].rearrange("p (t c) -> p t c", t=2),
                                      resid[:, g * TG + t:g * TG + t + 2, :], ALU.add).then_inc(s_yd, 1)

            def normalise(g):
                i = g % 2
                dve.wait_ge(s_ol[i], 32 * KC * (g // 2 + 1))
                wait(dve, s_y, 2 * (g - 1))
                for k in range(KC):
                    dve.tensor_tensor(on[i][:, k, :], ot[i][:, k, :], rb[i][:, k, :], ALU.mult).then_inc(s_on, 1)
            recip(0)
            normalise(0)
            normalise(1)
            recip(1)
            for g in range(NG):
                add_resid(g)
                if g + 2 < NG:
                    normalise(g + 2)
                if g == 0:
                    recip(2)

        @block.scalar
        def _(act):
            act.dma_start(idf[:, :], ident).then_inc(s_id, 16)
            act.dma_start(w1[:, :].rearrange("p (k n) -> p k n", k=KC), w1_t.rearrange("(k p) n -> p k n", p=P)).then_inc(s_w[0], 16)
            for dst, src in ((g_col, ln_g), (b_col, ln_b), (bq_col, bq), (b1_col, b1)):
                act.dma_start(dst[:, :], src).then_inc(s_col, 16)
            for dst, src in ((bv_row, bv), (bo_row, bo), (b2_row, b2)):
                act.dma_start(dst[:, :], src.to_broadcast((P, C))).then_inc(s_row, 16)

            def abs_sum(j, w):
                act.wait_ge(s_w[j], 16)
                act.activation(hid[:, KF // 2 * j:KF // 2 * (j + 1), :].rearrange("p f n -> p (f n)"), w[:, :], ACT.Abs,
                               accum_out=wabs[:, j:j + 1]).then_inc(s_wa, 1)

            abs_sum(0, w1)
            abs_sum(1, w2)
            act.wait_ge(s_col, 64)

            def group(g, first):
                act.wait_ge(s_tr, g + 1)
                wait(act, s_h, KF * g)
                for k in range(KC):
                    act.activation(x1[:, k, :], tr_x[k], ACT.Copy).then_inc(s_x1, 1)
                for k in range(KC):
                    act.wait_ge(s_xr, KC * g + k + 1)
                    act.activation(x2[:, k, :], xr[:, k, :], ACT.Copy).then_inc(s_x2, 1)
                if not first:
                    ffn_out(g - 1)
                    act.wait_ge(s_q3, g)
                    act.wait_ge(s_qs, 16 * KC * g)
                for k in range(KC):
                    act.wait_ge(s_q, KC * g + k + 1)
                    act.activation(qf[:, k, :], pq[k], ACT.Identity, bias=bq_col[:, k:k + 1]).then_inc(s_qa, 1)
                    act.activation(qp[:, k, 0, :], pq[k], ACT.Identity, bias=bq_col[:, k:k + 1]).then_inc(s_qa, 1)
                wait(act, s_h3, KF // 2 * g)
                for f in range(KF):
                    act.wait_ge(s_h, KF * g + f + 1)
                    act.activation(hid[:, f, :], pf[f % 2], ACT.Gelu, bias=b1_col[:, f:f + 1]).then_inc(s_g, 1)
                    if first and f == 0:
                        act.wait_ge(s_wd, 4)
                    act.activation(hp[0][:, f, :], pf[f % 2], ACT.Gelu, bias=b1_col[:, f:f + 1]).then_inc(s_g, 1)
                    if f % 4 == 3:
                        second(g, f // 2 - 1)

            def second(g, i):
                act.wait_ge(s_hr, KF // 2 * g + i + 1)
                if isinstance(g, int) and g == 0 and i == 0:
                    act.wait_ge(s_wd, 8)
                act.activation(hp[1][:, 2 * i:2 * i + 2, :], hid[:, 2 * i:2 * i + 2, :], ACT.Copy).then_inc(s_h2[0], 1)

            def ffn_out(g):
                for j in range(2):
                    act.wait_ge(s_f, 2 * g + j + 1)
                    if j == 0:
                        wait(act, s_ra, g)
                    act.activation(f2[:, 2 * j:2 * j + 2, :].rearrange("p t c -> p (t c)"), pf[j],
                                   ACT.Copy).then_inc(s_fe, 1)

            group(0, True)
            with act.Fori(1, NG) as g:
                group(g, False)
            ffn_out(NG - 1)

            def evacuate(h):
                act.wait_ge(s_pv, NBLK * (h + 1))
                wait(act, s_os, 16 * h)
                act.activation(o_sb, pv, ACT.Copy).then_inc(s_o, 1)

            def copy_max(h):
                act.wait_ge(s_mt, h + 1)
                wait(act, s_mr, 16 * h)
                act.activation(max_rows[:, :], pm[0:2 * NBLK, 0:P], ACT.Copy).then_inc(s_mc, 1)

            def head(h, first=False, last=False):
                for i in range(NE):
                    kb, c = i // NCH, i % NCH
                    act.wait_ge(s_b, NE * h + i + 1)
                    if c == 0 and not (first and kb < 2):
                        act.wait_ge(s_pv, NBLK * h + kb - 1)
                    act.activation(prob[kb % 2][:, c * BANK:(c + 1) * BANK], ring_bank(i, last), ACT.Exp,
                                   scale=SCALE).then_inc(s_e, 1)
                    if i == EVAC_AT and not first:
                        evacuate(h - 1)
                    if i == MAX_AT - 1 and not last:
                        copy_max(h + 1)
            copy_max(0)
            head(0, first=True)
            with act.Fori(1, NH - 1) as h:
                head(h)
            head(NH - 1, last=True)
            evacuate(NH - 1)

            for g in range(NG):
                act.wait_ge(s_yd, 2 * (g + 1))
                act.dma_start(out_v[g], y[g % 2]).then_inc(s_out[g % 2], 16)

        @block.tensor
        def _(pe):
            def ffn_down(g, t, between=None):
                for f in range(KF):
                    for i in range(3):
                        mm = pe.matmul(pf[t // 2][:, (t % 2) * C:(t % 2 + 1) * C], hp[i][:, f, t * P:(t + 1) * P],
                                       w2t[:, f, :], start=(f == 0 and i == 0), stop=(f == KF - 1 and i == 2))
                    if f == KF - 1 and t % 2:
                        mm.then_inc(s_f, 1)
                    if between and f % 2:
                        between()

            def abs_total(j):
                pe.wait_ge(s_wa, j + 1)
                pe.matmul(pf[j][:, 0:1], ones[:, :], wabs[:, j:j + 1], start=True, stop=True).then_inc(s_wp, 1)

            def group(g, between=None):
                pe.wait_ge(s_ln, 6 * g + 6)
                wait(pe, s_z, KC * g)
                wait(pe, s_xr, KC * g)
                for src, dst in ((xn, tr_x), (zn, tr_z)):
                    for k in range(KC):
                        for t in range(TG):
                            mm = pe.transpose(dst[k][:, t * P:(t + 1) * P], src[:, t, k * P:(k + 1) * P], idf[:, :])
                mm.then_inc(s_tr, 1)
                first = isinstance(g, int) and g == 0
                if first:
                    abs_total(1)
                else:
                    pe.wait_ge(s_h3, KF // 2 * g)
                    for t in range(TG):
                        ffn_down(g - 1, t, between if t >= TG // 2 else None)
                wait(pe, s_vd, TG * g)
                for o in range(KC):
                    for k in range(KC):
                        if o == 0:
                            pe.wait_ge(s_z, KC * g + k + 1)
                        mm = pe.matmul(pq[o], wq[:, k, o * P:(o + 1) * P], zt[:, k, :], start=(k == 0), stop=(k == KC - 1))
                    mm.then_inc(s_q, 1)
                if first:
                    pe.wait_ge(s_wd, 5)

                def hidden(f, between=None):
                    if f < 2:
                        wait(pe, s_fe, 2 * (g - 1) + f + 1)
                    else:
                        pe.wait_ge(s_g, 2 * (KF * g + f - 1))
                    for k in range(KC):
                        for i, part in enumerate((x1, x2, x3)):
                            mm = pe.matmul(pf[f % 2], w1t[:, k, f * P:(f + 1) * P], part[:, k, :],
                                           start=(k == 0 and i == 0), stop=(k == KC - 1 and i == 2))
                        if k == KC - 1:
                            mm.then_inc(s_h, 1)
                    if between:
                        between()
                pe.wait_ge(s_x3, KC * (g + 1))
                hidden(0)
                hidden(1)
                for f in range(2, KF):
                    hidden(f, between)
                if first:
                    pe.wait_ge(s_wv, 16)
                pe.wait_ge(s_qa, 2 * KC * (g + 1))
                for t in range(TG):
                    for k in range(KC):
                        mm = pe.matmul(pq[t // 2][:, (t % 2) * C:(t % 2 + 1) * C], zt[:, k, t * P:(t + 1) * P],
                                       wv[:, k, :], start=(k == 0), stop=(k == KC - 1))
                    if t % 2:
                        mm.then_inc(s_v, 1)

            pe.wait_ge(s_id, 16)
            pe.wait_ge(s_c, 1)
            abs_total(0)
            pe.wait_ge(s_wq, 16)
            group(0)
            with pe.Fori(1, NG - 1) as g:
                group(g)

            pe.wait_ge(s_pc, 3 + ROT)

            steps = iter([(0, a) for a in range(NA)] + [(1, a) for a in range(2)])
            calls = iter(range(3 * NA))

            def first_a():
                if EARLY <= next(calls) < TG * KF // 4:
                    return
                h, a = next(steps, (None, None))
                if h is None:
                    return
                if (h, a) == (0, 0):
                    pe.wait_ge(s_z, KC * NG)
                    pe.wait_ge(s_xr, KC * NG)
                if a == 0:
                    pe.wait_ge(s_ld[h], 96)
                a_step(pe, h, h, a)

            group(NG - 1, first_a)
            pe.wait_ge(s_h3, KF // 2 * NG)
            for t in range(TG):
                ffn_down(NG - 1, t, first_a)
            for _ in range(NA):
                first_a()
            pe.wait_ge(s_idb, 1)
            pe.wait_ge(s_vd, TG * NG)
            pe.wait_ge(s_fe, 2 * NG)
            max_transpose(pe, 0)
            for a in range(2, 3 * AHEAD):
                a_step(pe, 1, 1, a)
            pe_head(pe, 0, 0)
            n_it = (NH - 3) // ROT
            with pe.Fori(0, n_it) as j:
                for k in range(1, ROT + 1):
                    pe_head(pe, j, k)
            for h in range(1 + n_it * ROT, NH):
                pe_head(pe, 0, h)

            pe.wait_ge(s_wo, 16)
            for n in range(NT):
                project(pe, n // TG, n % TG)


def kernel(L0_attn_x, L0_attn_ln1_g, L0_attn_ln1_b, L0_attn_w_in, L0_attn_b_in, L0_attn_w_out, L0_attn_b_out,
           L0_ffn_W1, L0_ffn_b1, L0_ffn_W2, L0_ffn_b2):
    import numpy as np
    import concourse.bacc as bacc
    from concourse.bass_utils import run_bass_kernel_spmd

    c = L0_attn_x.shape[2]

    def array(a):
        return np.ascontiguousarray(np.asarray(a))

    def columns(v):
        return array(np.asarray(v).reshape(-1, P).T)

    w_in, b_in = np.asarray(L0_attn_w_in), np.asarray(L0_attn_b_in)
    arrays = {
        "x": array(L0_attn_x),
        "ln_g": columns(L0_attn_ln1_g), "ln_b": columns(L0_attn_ln1_b),
        "wq_t": array(w_in[0:c].T), "wv_t": array(w_in[2 * c:3 * c].T), "wo_t": array(np.asarray(L0_attn_w_out).T),
        "bq": columns(b_in[0:c]), "bv": array(b_in[None, 2 * c:3 * c]), "bo": array(np.asarray(L0_attn_b_out)[None, :]),
        "w1_t": array(np.asarray(L0_ffn_W1).T), "b1": columns(L0_ffn_b1),
        "w2_t": array(np.asarray(L0_ffn_W2).T), "b2": array(np.asarray(L0_ffn_b2)[None, :]),
        "ident": np.eye(P, dtype=np.float32),
    }
    nc = bacc.Bacc("TRN2", target_bir_lowering=False, num_devices=1)
    args = [nc.dram_tensor(f"in_{n}", a.shape, mybir.dt.from_np(a.dtype), kind="ExternalInput").ap()
            for n, a in arrays.items()]
    out = nc.dram_tensor("out", tuple(L0_attn_x.shape), F32, kind="ExternalOutput").ap()
    attention_ffn(nc, *args, out)
    r = run_bass_kernel_spmd(nc, [{f"in_{n}": a for n, a in arrays.items()}], core_ids=[0])
    return r.results[0]["out"]
```
